# Optimizing a Trainium2 kernel written in Bass

```python
import numpy as np
import jax
import jax.numpy as jnp

def _softmax(x, axis=-1):
    return jax.nn.softmax(x, axis=axis)

def _gelu(x):
    return jax.nn.gelu(x, approximate=True)

def _silu(x):
    return jax.nn.silu(x)

def _sigmoid(x):
    return jax.nn.sigmoid(x)

def _layernorm(x, axis=-1, eps=1e-05):
    m = jnp.mean(x, axis=axis, keepdims=True)
    v = jnp.var(x, axis=axis, keepdims=True)
    return (x - m) / jnp.sqrt(v + eps)

def _scatter_add(tgt, idx, src, axis=0):
    return tgt.at[idx].add(src)

def _segment_sum(src, seg, n):
    return jax.ops.segment_sum(src, seg, n)
kernel_name = 'mk_early_fusion_embed_d1_tok_img768_r4_34a771'

def setup_inputs(seed: int=0):
    np.random.seed(seed)
    _w = jnp.asarray

    def _rec_inputs():
        import jax
        import jax.numpy as jnp
        _rk = jax.random.key(seed)
        x = -0.000222058 + 0.999998 * jax.random.normal(jax.random.fold_in(_rk, 1), (8, 3, 518, 518), jnp.float32)
        x_txt = jax.random.randint(jax.random.fold_in(_rk, 51), (8, 32), 0, 12564, jnp.int32)
        return (x, x_txt)
    x, x_txt = _rec_inputs()

    def _L0_tok_setup():
        import jax, jax.numpy as jnp
        import numpy as np
        from jax import lax
        HIDDEN = 192
        C_IN = 3
        PATCH = 16
        SIDE = 32
        NUM_PATCHES = SIDE * SIDE

        def _position_ids(nb_h, nb_w):
            boundaries = np.arange(1.0 / SIDE, 1.0, 1.0 / SIDE, dtype=np.float32)
            frac_h = np.arange(0.0, 1.0 - 1e-06, 1.0 / nb_h, dtype=np.float32)
            frac_w = np.arange(0.0, 1.0 - 1e-06, 1.0 / nb_w, dtype=np.float32)
            bh = np.searchsorted(boundaries, frac_h, side='right')
            bw = np.searchsorted(boundaries, frac_w, side='right')
            return jnp.asarray((bh[:, None] * SIDE + bw).reshape(-1), dtype=jnp.int32)
        key = jax.random.key(seed)
        k1, k2, k3 = jax.random.split(key, 3)
        pixel_values = jax.random.normal(k1, (32, C_IN, 128, 128), dtype=jnp.float32)
        conv_w = jax.random.normal(k2, (HIDDEN, C_IN, PATCH, PATCH), dtype=jnp.float32) * 0.02
        conv_b = jnp.zeros((HIDDEN,), dtype=jnp.float32)
        pos_table = jax.random.normal(k3, (NUM_PATCHES, HIDDEN), dtype=jnp.float32) * 0.02
        return {'pixel_values': pixel_values, 'conv_w': conv_w, 'conv_b': conv_b, 'pos_table': pos_table}
    _L0_tok_all = _L0_tok_setup()
    _L0_tok_in = {k: v for k, v in _L0_tok_all.items() if k in ('conv_w', 'conv_b', 'pos_table')}
    del _L0_tok_all

    def _L0_txt_setup():
        import jax, jax.numpy as jnp
        import numpy as np
        VOCAB = 50257
        EMBED_DIM = 192
        key = jax.random.key(seed)
        k1, k2 = jax.random.split(key)
        x = jax.random.randint(k1, (8, 512), 0, VOCAB, dtype=jnp.int64 if jax.config.jax_enable_x64 else jnp.int32)
        weight = jax.random.normal(k2, (EMBED_DIM, VOCAB), dtype=jnp.float32)
        return {'x': x, 'weight': weight}
    _L0_txt_all = _L0_txt_setup()
    _L0_txt_in = {k: v for k, v in _L0_txt_all.items() if k in ('weight',)}
    del _L0_txt_all

    def _L0_attn_setup():
        import jax, jax.numpy as jnp
        import numpy as np
        B, S, D, DC, H = (4, 512, 192, 96, 12)
        HD = DC // H
        key = jax.random.key(seed)
        ks = jax.random.split(key, 8)
        std = 0.02
        return {'hidden_states': jax.random.normal(ks[0], (B, S, D), dtype=jnp.float32), 'W_attn': jax.random.normal(ks[1], (D, 3 * D), dtype=jnp.float32) * std, 'b_attn': jnp.zeros((3 * D,), dtype=jnp.float32), 'P_q': jax.random.normal(ks[2], (D, DC), dtype=jnp.float32) * std, 'P_k': jax.random.normal(ks[3], (D, DC), dtype=jnp.float32) * std, 'P_v': jax.random.normal(ks[4], (D, DC), dtype=jnp.float32) * std, 'W_back': jax.random.normal(ks[5], (DC, D), dtype=jnp.float32) * std, 'W_proj': jax.random.normal(ks[6], (D, D), dtype=jnp.float32) * std, 'b_proj': jnp.zeros((D,), dtype=jnp.float32)}
    _L0_attn_all = _L0_attn_setup()
    _L0_attn_in = {k: v for k, v in _L0_attn_all.items() if k in ('W_attn', 'b_attn', 'P_q', 'P_k', 'P_v', 'W_back', 'W_proj', 'b_proj')}
    del _L0_attn_all

    def _L0_ffn_setup():
        import jax, jax.numpy as jnp
        import numpy as np
        EMBED_DIM = 192
        FF_MULT = 4
        HIDDEN = EMBED_DIM * FF_MULT
        BATCH, SEQ = (32, 256)
        EPS = 1e-06

        def rmsnorm(x, g):
            return x * jax.lax.rsqrt(jnp.mean(x * x, axis=-1, keepdims=True) + EPS) * g

        def act_quant(x):
            scale = 127.0 / jnp.clip(jnp.max(jnp.abs(x), axis=-1, keepdims=True), 1e-05, None)
            return jnp.clip(jnp.round(x * scale), -128.0, 127.0) / scale

        def weight_quant(w):
            scale = 1.0 / jnp.clip(jnp.mean(jnp.abs(w)), 1e-05, None)
            return jnp.clip(jnp.round(w * scale), -1.0, 1.0) / scale

        def bitlinear(x, w, g):
            xn = rmsnorm(x, g)
            xq = xn + jax.lax.stop_gradient(act_quant(xn) - xn)
            wq = w + jax.lax.stop_gradient(weight_quant(w) - w)
            return jnp.einsum('bsd,fd->bsf', xq, wq)
        key = jax.random.key(seed)
        k1, k2, k3 = jax.random.split(key, 3)
        x = jax.random.normal(k1, (BATCH, SEQ, EMBED_DIM), dtype=jnp.float32)
        w1 = jax.random.normal(k2, (HIDDEN, EMBED_DIM), dtype=jnp.float32) * 0.02
        w2 = jax.random.normal(k3, (EMBED_DIM, HIDDEN), dtype=jnp.float32) * 0.02
        g1 = jnp.ones((EMBED_DIM,), dtype=jnp.float32)
        g2 = jnp.ones((HIDDEN,), dtype=jnp.float32)
        return {'x': x, 'w1': w1, 'g1': g1, 'w2': w2, 'g2': g2}
    _L0_ffn_all = _L0_ffn_setup()
    _L0_ffn_in = {k: v for k, v in _L0_ffn_all.items() if k in ('w1', 'g1', 'w2', 'g2')}
    del _L0_ffn_all
    return {'x': x, 'x_txt': x_txt, 'L0_tok_conv_w': _L0_tok_in['conv_w'], 'L0_tok_conv_b': _L0_tok_in['conv_b'], 'L0_tok_pos_table': _L0_tok_in['pos_table'], 'L0_txt_weight': _L0_txt_in['weight'], 'L0_attn_W_attn': _L0_attn_in['W_attn'], 'L0_attn_b_attn': _L0_attn_in['b_attn'], 'L0_attn_P_q': _L0_attn_in['P_q'], 'L0_attn_P_k': _L0_attn_in['P_k'], 'L0_attn_P_v': _L0_attn_in['P_v'], 'L0_attn_W_back': _L0_attn_in['W_back'], 'L0_attn_W_proj': _L0_attn_in['W_proj'], 'L0_attn_b_proj': _L0_attn_in['b_proj'], 'L0_ffn_w1': _L0_ffn_in['w1'], 'L0_ffn_g1': _L0_ffn_in['g1'], 'L0_ffn_w2': _L0_ffn_in['w2'], 'L0_ffn_g2': _L0_ffn_in['g2']}

def reference(x, x_txt, L0_tok_conv_w, L0_tok_conv_b, L0_tok_pos_table, L0_txt_weight, L0_attn_W_attn, L0_attn_b_attn, L0_attn_P_q, L0_attn_P_k, L0_attn_P_v, L0_attn_W_back, L0_attn_W_proj, L0_attn_b_proj, L0_ffn_w1, L0_ffn_g1, L0_ffn_w2, L0_ffn_g2):
    import jax
    import jax.numpy as jnp

    def _L0_tok_ref(pixel_values, conv_w, conv_b, pos_table):
        import jax, jax.numpy as jnp
        import numpy as np
        from jax import lax
        HIDDEN = 192
        C_IN = 3
        PATCH = 16
        SIDE = 32
        NUM_PATCHES = SIDE * SIDE

        def _position_ids(nb_h, nb_w):
            boundaries = np.arange(1.0 / SIDE, 1.0, 1.0 / SIDE, dtype=np.float32)
            frac_h = np.arange(0.0, 1.0 - 1e-06, 1.0 / nb_h, dtype=np.float32)
            frac_w = np.arange(0.0, 1.0 - 1e-06, 1.0 / nb_w, dtype=np.float32)
            bh = np.searchsorted(boundaries, frac_h, side='right')
            bw = np.searchsorted(boundaries, frac_w, side='right')
            return jnp.asarray((bh[:, None] * SIDE + bw).reshape(-1), dtype=jnp.int32)
        B, _, H, W = pixel_values.shape
        nb_h, nb_w = (H // PATCH, W // PATCH)
        patches = lax.conv_general_dilated(pixel_values, conv_w, window_strides=(PATCH, PATCH), padding='VALID', dimension_numbers=('NCHW', 'OIHW', 'NCHW'))
        patches = patches + conv_b[None, :, None, None]
        embeddings = patches.reshape(B, HIDDEN, nb_h * nb_w).transpose(0, 2, 1)
        pos_ids = _position_ids(nb_h, nb_w)
        pos_emb = pos_table[pos_ids]
        return embeddings + pos_emb[None, :, :]

    def _L0_txt_ref(x, weight):
        import jax, jax.numpy as jnp
        import numpy as np
        VOCAB = 50257
        EMBED_DIM = 192
        return jnp.take(weight.T, x, axis=0)

    def _L0_attn_ref(hidden_states, W_attn, b_attn, P_q, P_k, P_v, W_back, W_proj, b_proj):
        import jax, jax.numpy as jnp
        import numpy as np
        B, S, D, DC, H = (4, 512, 192, 96, 12)
        HD = DC // H
        b, s, _ = hidden_states.shape
        qkv = hidden_states @ W_attn + b_attn
        q, k, v = jnp.split(qkv, 3, axis=-1)
        q = q @ P_q
        k = k @ P_k
        v = v @ P_v
        split = lambda t: t.reshape(b, s, H, HD).transpose(0, 2, 1, 3)
        qh, kh, vh = (split(q), split(k), split(v))
        scores = jnp.einsum('bhqd,bhkd->bhqk', qh, kh) / jnp.sqrt(jnp.float32(HD))
        causal = jnp.tril(jnp.ones((s, s), dtype=scores.dtype))
        scores = scores * causal + -10000.0 * (1.0 - causal)
        weights = jax.nn.softmax(scores, axis=-1)
        ctx = jnp.einsum('bhqk,bhkd->bhqd', weights, vh)
        ctx = ctx.transpose(0, 2, 1, 3).reshape(b, s, DC)
        out = ctx @ W_back
        out = out @ W_proj + b_proj
        return out

    def _L0_ffn_ref(x, w1, g1, w2, g2):
        import jax, jax.numpy as jnp
        import numpy as np
        EMBED_DIM = 192
        FF_MULT = 4
        HIDDEN = EMBED_DIM * FF_MULT
        BATCH, SEQ = (32, 256)
        EPS = 1e-06

        def rmsnorm(x, g):
            return x * jax.lax.rsqrt(jnp.mean(x * x, axis=-1, keepdims=True) + EPS) * g

        def act_quant(x):
            scale = 127.0 / jnp.clip(jnp.max(jnp.abs(x), axis=-1, keepdims=True), 1e-05, None)
            return jnp.clip(jnp.round(x * scale), -128.0, 127.0) / scale

        def weight_quant(w):
            scale = 1.0 / jnp.clip(jnp.mean(jnp.abs(w)), 1e-05, None)
            return jnp.clip(jnp.round(w * scale), -1.0, 1.0) / scale

        def bitlinear(x, w, g):
            xn = rmsnorm(x, g)
            xq = xn + jax.lax.stop_gradient(act_quant(xn) - xn)
            wq = w + jax.lax.stop_gradient(weight_quant(w) - w)
            return jnp.einsum('bsd,fd->bsf', xq, wq)
        h = jax.nn.gelu(bitlinear(x, w1, g1), approximate=False)
        return bitlinear(h, w2, g2)
    h = _L0_tok_ref(x, L0_tok_conv_w, L0_tok_conv_b, L0_tok_pos_table)
    h = jnp.concatenate([h, _L0_txt_ref(x_txt, L0_txt_weight)], axis=1)
    h = h + _L0_attn_ref(_layernorm(h, axis=-1), L0_attn_W_attn, L0_attn_b_attn, L0_attn_P_q, L0_attn_P_k, L0_attn_P_v, L0_attn_W_back, L0_attn_W_proj, L0_attn_b_proj)
    h = h + _L0_ffn_ref(_layernorm(h, axis=-1), L0_ffn_w1, L0_ffn_g1, L0_ffn_w2, L0_ffn_g2)
    return h

_drawn_inputs = setup_inputs


def setup_inputs(seed=0):
    import zlib

    import numpy as np

    out = dict(_drawn_inputs(seed))
    spreads = {'L0_tok_conv_b': (0.0, 0.1),
     'L0_attn_b_attn': (0.0, 0.8),
     'L0_attn_b_proj': (0.0, 0.8),
     'L0_ffn_g1': (1.0, 0.6),
     'L0_ffn_g2': (1.0, 0.6)}
    factors = {'L0_attn_W_attn': 8.0,
     'L0_attn_P_q': 8.0,
     'L0_attn_P_k': 8.0,
     'L0_attn_P_v': 8.0,
     'L0_attn_W_back': 8.0,
     'L0_attn_W_proj': 8.0}
    for name, (base, spread) in spreads.items():
        noise = np.random.default_rng([zlib.crc32(name.encode()), seed]).standard_normal(out[name].shape)
        drawn = base * np.exp(spread * noise) if base else spread * noise
        out[name] = jnp.asarray(drawn.astype(out[name].dtype))
    for name, factor in factors.items():
        out[name] = (out[name] * factor).astype(out[name].dtype)
    return out
```

```python
from contextlib import ExitStack

import concourse.bass as bass
from concourse import mybir

F32 = mybir.dt.float32
BF16 = mybir.dt.bfloat16
I32 = mybir.dt.int32
ALU = mybir.AluOpType
ACT = mybir.ActivationFunctionType
AX_X = mybir.AxisListType.X

P = 128
B, C_IN, IMG, PATCH = 8, 3, 518, 16
SIDE = IMG // PATCH
NPATCH = SIDE * SIDE
NTXT = 32
S = NPATCH + NTXT
D, DC, H = 192, 96, 12
HD = DC // H
DH = D // 2
DFF = 768
KC = C_IN * PATCH * PATCH
KT = KC // P
NT = NPATCH // P
NTT = NT + 1
GRP = 4
W = GRP * P
HALVES = NT // GRP
NGRP = B * HALVES
TXT_TILES = B * NTXT // P
NPART = 6
KROWS = NPART * HD
MROW = 64
KALL = MROW + 3
VW = HD + 1
TOK = B * S
CT = TOK // P
FT = DFF // P
UPW = DFF // 2
NEG = -1.0e30
MAGIC = 1.5 * 2.0 ** 23
LN_EPS, RMS_EPS, Q_EPS = 1e-5, 1e-6, 1e-5
PARTS_Q = (0, 1, 2, 0, 1, 0)
PARTS_K = (0, 0, 0, 1, 1, 2)


def s2_chunks(j):
    left = S - P * j
    n = -(-left // 512)
    w = -(-left // (n * 32)) * 32
    return [(c * w, min(w, left - c * w)) for c in range(n)]


CHUNKS = [(j, a, w) for j in range(NTT) for a, w in s2_chunks(j)]
NS2 = len(CHUNKS)
DONE_AT = [max(n for n, c in enumerate(CHUNKS) if c[0] == j) + 1 for j in range(NTT)]
POFF = [sum(S - P * i for i in range(j)) for j in range(NTT)]
PCOLS = POFF[NT] + NTXT
S1_USES = [(i, 0, P * (i + 1)) for i in range(NT)] + [(NT, 0, NPATCH), (NT, NPATCH, NTXT)]
NS1 = len(S1_USES) + 2
RING2, RING3 = 2, 3
CONSTANTS = 7
NSETUP = 14
SUM_STEPS = 9 + NT + 2
WEIGHT_STEPS = SUM_STEPS + 16
FIRST, SECOND = 11, 9
NORM = 6


def early_fusion_kernel(nc, xT, idx, conv_w, conv_b, pos, emb, w_attn, p_q, p_k, p_v, w_back, w_proj, b_proj,
                        w1, g1, w2, g2, out):
    q_dram = nc.dram_tensor("q_stacked", (B, DC, NPART, S), BF16, kind="Internal").ap()
    k_dram = nc.dram_tensor("k_stacked", (B, DC, NPART, S), BF16, kind="Internal").ap()
    v_dram = nc.dram_tensor("v_tiles", (B, H, P, NTT, VW), F32, kind="Internal").ap()
    h_dram = nc.dram_tensor("embedded", (B, S, D), F32, kind="Internal").ap()
    h2_dram = nc.dram_tensor("attended", (TOK, D), F32, kind="Internal").ap()

    with ExitStack() as ctx:
        def sb(name, shape, dt=F32):
            return ctx.enter_context(nc.sbuf_tensor(name, shape, dt))

        def sem(name):
            return ctx.enter_context(nc.semaphore(name))

        psum = ctx.enter_context(nc.psum_tensor("psum", [P, 8, 512], F32))

        identf = sb("identf", [P, P])
        ident = sb("ident", [P, P], BF16)
        tri = sb("tri", [P, P], BF16)
        ones = sb("ones", [P, P])
        halfneg = sb("halfneg", [P, GRP])
        idx_sb = sb("idx_sb", [P, TXT_TILES], I32)
        txt = sb("txt", [P, TXT_TILES, D])
        convw = sb("convw", [P, KT, D])
        posb = sb("posb", [P, NT, D])
        convb = sb("convb", [P, D])
        wat = sb("wat", [DH, 6, D + 1])
        pqkv = sb("pqkv", [DH, 6, DC])
        wqkv = sb("wqkv", [DH + 1, 2, 3, DC])
        wbt = sb("wbt", [DH, 2, DC])
        wpj = sb("wpj", [DH, 2, D])
        wout = sb("wout", [DC + 1, D])
        w1f = sb("w1f", [DH, 2, DFF])
        w2f = sb("w2f", [P, FT, D])
        w1q = sb("w1q", [DH, 2, DFF], BF16)
        w2q = sb("w2q", [P, FT, D], BF16)
        g1b = sb("g1b", [P, D])
        g2b = sb("g2b", [P, DFF])
        wsum = sb("wsum", [P, 2])
        wscale = sb("wscale", [P, 2])
        winv = sb("winv", [P, 2])
        wdq = sb("wdq", [P, 2])

        xt = sb("xt", [P, RING2, KT, W])
        hA = sb("hA", [P, RING2, GRP, D])
        bnA = sb("bnA", [P, GRP, 6])
        mvA = sb("mvA", [P, GRP, 2])
        veA = sb("veA", [P, GRP])
        rsA = sb("rsA", [P, GRP])
        zA = sb("zA", [P, GRP, D])
        zT = sb("zT", [DH + 1, 2, W])
        split = sb("split", [DC, 2, 3, W], BF16)
        rest = sb("rest", [DC, 2, W])
        vA = sb("vA", [P, H, GRP, VW])

        qs = sb("qs", [P, RING2, S], BF16)
        ks = sb("ks", [P, RING2, S], BF16)
        vs = sb("vs", [P, RING2, NTT, VW])
        pT = sb("pT", [P, RING2, PCOLS])
        nmax = sb("nmax", [P, NTT + 1])
        nmrest = sb("nmrest", [P, NTT])
        nmparts = sb("nmparts", [P, NTT, 3], BF16)
        rden = sb("rden", [P, NTT])
        cx = sb("cx", [P, NTT, DC])
        cxT = sb("cxT", [DC + 1, RING3, P])
        hB = sb("hB", [P, NTT, D])
        h2B = sb("h2B", [P, RING3, D])

        hC = sb("hC", [P, RING3, D])
        bnC = sb("bnC", [P, 6])
        mvC = sb("mvC", [P, 2])
        stC = sb("stC", [P, RING3, 16])
        uC = sb("uC", [P, D])
        tC = sb("tC", [P, D])
        xqC = sb("xqC", [P, D], BF16)
        x1T = sb("x1T", [DH, 2, P], BF16)
        gl = sb("gl", [P, RING3, DFF])
        sq = sb("sq", [P, DFF])
        uF = sb("uF", [P, DFF])
        tF = sb("tF", [P, DFF])
        xqF = sb("xqF", [P, DFF], BF16)
        x2T = sb("x2T", [P, FT, P], BF16)
        oC = sb("oC", [P, RING3, D])

        idx_loaded, gathered = sem("idx_loaded"), sem("gathered")
        setup_loaded = sem("setup_loaded")
        const_step = sem("const_step")
        weights_step = sem("weights_step")
        folded = sem("folded")
        x_loaded = [sem("x_loaded0"), sem("x_loaded1")]
        conv_done, h_ready = sem("conv_done"), sem("h_ready")
        stats_done, aggr_done = sem("stats_done"), sem("aggr_done")
        eps_added, rstd_ready = sem("eps_added"), sem("rstd_ready")
        z_ready, zT_done, zT_copied = sem("z_ready"), sem("zT_done"), sem("zT_copied")
        qk_done, v_done = sem("qk_done"), sem("v_done")
        hi_ready, rest_ready = sem("hi_ready"), sem("rest_ready")
        mid_ready, lo_ready = sem("mid_ready"), sem("lo_ready")
        v_copied = sem("v_copied")
        h_stored = [sem("h_stored0"), sem("h_stored1")]
        qk_stored, v_stored = sem("qk_stored"), sem("v_stored")
        qkv_loaded = [sem("qkv_loaded0"), sem("qkv_loaded1")]
        hB_loaded = sem("hB_loaded")
        s1_done, s1_read = sem("s1_done"), sem("s1_read")
        parts_step, parts_ready = sem("parts_step"), sem("parts_ready")
        s2_done, exp_done = sem("s2_done"), sem("exp_done")
        av_done, rden_ready, av_read = sem("av_done"), sem("rden_ready"), sem("av_read")
        cxT_done, cxT_copied = sem("cxT_done"), sem("cxT_copied")
        proj_done, h2_ready = sem("proj_done"), sem("h2_ready")
        h2_stored = [sem(f"h2_stored{i}") for i in range(RING3)]
        hC_loaded = [sem(f"hC_loaded{i}") for i in range(RING3)]
        first_step = sem("first_step")
        second_step = sem("second_step")
        norm_step = sem("norm_step")
        scaled, rms2_step = sem("scaled"), sem("rms2_step")
        x1T_done, x1T_copied, up_done, gelu_done = sem("x1T_done"), sem("x1T_copied"), sem("up_done"), sem("gelu_done")
        x2T_done, x2T_copied, down_done = sem("x2T_done"), sem("x2T_copied"), sem("down_done")
        out_stored = [sem(f"out_stored{i}") for i in range(RING3)]
        waits_met = sem("waits_met")

        block = ctx.enter_context(nc.Block())

        def own_wait(eng):
            eng.sem_inc(waits_met, 1)

        def stage_c(eng, first, second):
            first(0, 0, 0)
            with eng.Fori(0, CT // RING3 - 1) as i:
                for k in range(RING3):
                    first(i * RING3 + k + 1, (k + 1) % RING3, i + (k + 1) // RING3)
                    second(i * RING3 + k, k, i)
            for t in range(CT - RING3, CT):
                if t < CT - 1:
                    first(t + 1, (t + 1) % RING3, (t + 1) // RING3)
                second(t, t % RING3, t // RING3)

        def stage_b(eng, before, head_step, after):
            with eng.Fori(0, B) as b:
                before(b)
                with eng.Fori(0, H // 2 - 1) as pair:
                    for par in range(RING2):
                        head_step(b, pair, par, True)
                head_step(b, H // 2 - 1, 0, True)
                head_step(b, H // 2 - 1, 1, False)
                after(b)

        convP = [psum[:, i, 0:D] for i in range(RING2)]
        zTP = [psum[0:DH, 2 + a, :] for a in range(2)]
        qkP = [psum[0:DC, 4 + i, :] for i in range(2)]
        vP = psum[:, 6, 0:GRP * DC].rearrange("p (t c) -> p t c", t=GRP)
        s1P = [psum[:, 2 * i:2 * i + 2, :].rearrange("p a b -> p (a b)") for i in range(RING2)]
        s2P = [psum[:, 4 + i, :] for i in range(RING3)]
        avP = psum[:, 7, 0:NTT * VW].rearrange("p (t c) -> p t c", t=NTT)
        cxTP = [psum[0:DC, 4 + i, 0:P] for i in range(RING3)]
        projP = [psum[:, i, 0:D] for i in range(RING3)]
        x1TP = psum[0:DH, 0, 0:P].bitcast(BF16).rearrange("p (a t) -> p a t", a=2)
        upP = psum[:, 1:3, 0:UPW]
        x2TP = psum[:, 3, 0:FT * P // 2].bitcast(BF16).rearrange("p (f t) -> p f t", f=FT)
        downP = psum[:, 4, 0:D]
        foldP = [psum[0:DH + 1, a, 0:3 * DC].rearrange("p (m c) -> p m c", m=3) for a in range(2)]
        woutP = psum[0:DC, 2, 0:D]
        wsumP = psum[:, 3, 0:2]

        @block.sync
        def _(sp):
            sp.dma_start(idx_sb[:], idx).then_inc(idx_loaded, 16)
            sp.dma_start(wat[:], w_attn).then_inc(setup_loaded, 16)
            sp.dma_start(pqkv[:, 0:2, :], p_q).then_inc(setup_loaded, 16)
            sp.dma_start(pqkv[:, 2:4, :], p_k).then_inc(setup_loaded, 16)
            sp.dma_start(pqkv[:, 4:6, :], p_v).then_inc(setup_loaded, 16)
            sp.dma_start(convw[:], conv_w).then_inc(setup_loaded, 16)
            sp.dma_start(xt[:, 0], xT[0]).then_inc(x_loaded[0], 16)
            sp.dma_start(posb[:], pos).then_inc(setup_loaded, 16)
            sp.dma_start(convb[:], conv_b.partition_broadcast(P)).then_inc(setup_loaded, 16)
            sp.dma_start(g1b[:], g1.partition_broadcast(P)).then_inc(setup_loaded, 16)
            sp.dma_start(g2b[:], g2.partition_broadcast(P)).then_inc(setup_loaded, 16)
            sp.dma_start(wbt[:], w_back).then_inc(setup_loaded, 16)
            sp.dma_start(wpj[:], w_proj).then_inc(setup_loaded, 16)
            sp.dma_start(wout[DC:DC + 1, :], b_proj).then_inc(setup_loaded, 16)
            sp.dma_start(w1f[:], w1).then_inc(setup_loaded, 16)
            sp.dma_start(w2f[:], w2).then_inc(setup_loaded, 16)
            sp.dma_start(xt[:, 1], xT[1]).then_inc(x_loaded[1], 16)

            def store_group(g, b, half, tiles):
                lo, hi = half * W, half * W + W
                if b is None:
                    sp.wait_ge(h_ready, RING2 + NGRP * GRP + tiles)
                    for t in range(tiles):
                        for bb in range(GRP):
                            sp.dma_start(h_dram[GRP * t + bb, NPATCH:S, :],
                                         hA[NTXT * bb:NTXT * bb + NTXT, 0, t, :]).then_inc(h_stored[0], 16)
                else:
                    sp.wait_ge(h_ready, g * GRP + RING2 + tiles)
                    sp.dma_start(h_dram[bass.ds(b, 1), lo:hi, :].rearrange("a (t p) d -> (a p) t d", p=P),
                                 hA[:, half]).then_inc(h_stored[half], 16)
                sp.wait_ge(hi_ready, g * 2 + 2)
                sp.wait_ge(mid_ready, g * 2 + 2)
                sp.wait_ge(lo_ready, g * 2 + 2)
                for which, dram, parts in ((0, q_dram, PARTS_Q), (1, k_dram, PARTS_K)):
                    for slot in range(NPART):
                        src = split[:, which, parts[slot], :]
                        if b is None:
                            sp.dma_start(dram[:, :, slot, NPATCH:S].rearrange("b p t -> p b t"),
                                         src[:, 0:B * NTXT].rearrange("p (b t) -> p b t", b=B)).then_inc(qk_stored, 16)
                        else:
                            sp.dma_start(dram[bass.ds(b, 1), :, slot, lo:hi].rearrange("a p t -> (a p) t"),
                                         src).then_inc(qk_stored, 16)
                sp.wait_ge(v_copied, g + 2)
                if b is None:
                    for t in range(tiles):
                        for bb in range(GRP):
                            sp.dma_start(v_dram[GRP * t + bb, :, 0:NTXT, NT, :].rearrange("h p c -> p h c"),
                                         vA[NTXT * bb:NTXT * bb + NTXT, :, t, :]).then_inc(v_stored, 16)
                else:
                    sp.dma_start(v_dram[bass.ds(b, 1), :, :, half * GRP:half * GRP + GRP, :]
                                 .rearrange("a h p t c -> (a p) h (t c)"),
                                 vA[:].rearrange("p h t c -> p h (t c)")).then_inc(v_stored, 16)

            def batch_stores(b, prefetch):
                for half in range(HALVES):
                    g = b * HALVES + half
                    if prefetch:
                        sp.wait_ge(conv_done, g * GRP + GRP)
                        sp.dma_start(xt[:, half], xT[bass.ds(g + RING2, 1)].rearrange("a p k t -> (a p) k t")
                                     ).then_inc(x_loaded[half], 16)
                    store_group(g, b, half, GRP)

            with sp.Fori(0, B - 1) as b:
                batch_stores(b, True)
            batch_stores(B - 1, False)
            store_group(NGRP, None, 0, TXT_TILES)

            sp.wait_ge(h_stored[0], 16 * (1 + B + B))
            sp.wait_ge(h_stored[1], 16 * (1 + B))
            sp.wait_ge(qk_stored, 16 * 2 * NPART * (1 + NGRP + 1))
            sp.wait_ge(v_stored, 16 * (1 + NGRP + B))

            with sp.Fori(0, B) as b:
                sp.wait_ge(h2_ready, b * NTT + RING3)
                sp.dma_start(hB[:, 0:NT, :], h_dram[bass.ds(b, 1), 0:NPATCH, :].rearrange("a (t p) d -> (a p) t d", p=P)
                             ).then_inc(hB_loaded, 16)
                sp.dma_start(hB[0:NTXT, NT, :], h_dram[bass.ds(b, 1), NPATCH:S, :].rearrange("a t d -> (a t) d")
                             ).then_inc(hB_loaded, 16)
                with sp.Fori(0, H // 2) as pair:
                    for par in range(2):
                        head = pair * 2 + par
                        sp.wait_ge(av_done, b * H + head + 1)
                        sp.dma_start(qs[0:KROWS, par, :],
                                     q_dram[bass.ds(b, 1), bass.ds(head * HD, HD)].rearrange("a r s t -> (a r s) t")
                                     ).then_inc(qkv_loaded[par], 16)
                        sp.dma_start(ks[0:KROWS, par, :],
                                     k_dram[bass.ds(b, 1), bass.ds(head * HD, HD)].rearrange("a r s t -> (a r s) t")
                                     ).then_inc(qkv_loaded[par], 16)
                        sp.dma_start(vs[:, par, 0:NT, :],
                                     v_dram[bass.ds(b, 1), bass.ds(head, 1), :, 0:NT, :]
                                     .rearrange("a h p t c -> (a h p) t c")).then_inc(qkv_loaded[par], 16)
                        sp.dma_start(vs[0:NTXT, par, NT, :],
                                     v_dram[bass.ds(b, 1), bass.ds(head, 1), 0:NTXT, NT, :]
                                     .rearrange("a h p c -> (a h p) c")).then_inc(qkv_loaded[par], 16)
                for t in range(NTT):
                    rows = P if t < NT else NTXT
                    sp.wait_ge(h2_ready, b * NTT + t + 1 + RING3)
                    sp.dma_start(h2_dram[bass.ds(b * S + t * P, rows), :],
                                 h2B[0:rows, t % RING3, :]).then_inc(h2_stored[t % RING3], 16)

            for k in range(RING3):
                sp.wait_ge(h2_stored[k], 16 * (1 + B * NTT // RING3))

            def load_tile(row, k):
                sp.dma_start(hC[:, k, :], h2_dram[row, :]).then_inc(hC_loaded[k], 16)

            for k in range(RING3):
                load_tile(slice(P * k, P * k + P), k)
            with sp.Fori(0, CT // RING3 - 1) as i:
                for k in range(RING3):
                    t = i * RING3 + k
                    sp.wait_ge(second_step, t * SECOND + 2 * SECOND)
                    sp.dma_start(out[bass.ds(t * P, P), :], oC[:, k, :]).then_inc(out_stored[k], 16)
                    load_tile(bass.ds((t + RING3) * P, P), k)
            for k in range(RING3):
                t = CT - RING3 + k
                sp.wait_ge(second_step, t * SECOND + 2 * SECOND)
                sp.dma_start(out[t * P:t * P + P, :], oC[:, k, :]).then_inc(out_stored[k], 16)
            for k in range(RING3):
                sp.wait_ge(out_stored[k], 16 * (1 + CT // RING3))

        @block.gpsimd
        def _(pool):
            for s, n in ((h_ready, RING2), (h_stored[0], 16), (h_stored[1], 16), (zT_done, 1), (zT_copied, 2), (v_done, 1),
                         (rest_ready, 2), (v_copied, 1), (qk_stored, 16 * 2 * NPART), (v_stored, 16),
                         (av_done, RING2), (s1_read, RING2), (exp_done, RING3), (av_read, 1), (cxT_done, 1),
                         (cxT_copied, RING3), (proj_done, RING3), (h2_ready, RING3), *((q, 16) for q in h2_stored),
                         *((q, 16) for q in out_stored), (x1T_done, 1), (x1T_copied, 1), (gelu_done, 1), (x2T_done, 1),
                         (x2T_copied, 1), (second_step, SECOND)):
                pool.sem_inc(s, n)
            nc.gpsimd.memset(ident[:], 0.0).then_inc(const_step, 1)
            nc.gpsimd.memset(identf[:], 0.0).then_inc(const_step, 1)
            nc.gpsimd.memset(tri[:], 0.0).then_inc(const_step, 1)
            nc.gpsimd.memset(halfneg[:], -0.5).then_inc(const_step, 1)
            pool.wait_ge(const_step, 4)
            nc.gpsimd.affine_select(out=ident[:], in_=ident[:], compare_op=ALU.not_equal, fill=1.0, base=0,
                                    pattern=[[-1, P]], channel_multiplier=1).then_inc(const_step, 1)
            nc.gpsimd.affine_select(out=identf[:], in_=identf[:], compare_op=ALU.not_equal, fill=1.0, base=0,
                                    pattern=[[-1, P]], channel_multiplier=1).then_inc(const_step, 1)
            nc.gpsimd.affine_select(out=tri[:], in_=tri[:], compare_op=ALU.is_ge, fill=NEG, base=0,
                                    pattern=[[1, P]], channel_multiplier=-1).then_inc(const_step, 1)
            pool.wait_ge(idx_loaded, 16)
            for t in range(TXT_TILES):
                nc.gpsimd.indirect_dma_start(out=txt[:, t, :], out_offset=None, in_=emb,
                                             in_offset=bass.IndirectOffsetOnAxis(ap=idx_sb[:, t:t + 1], axis=0)
                                             ).then_inc(gathered, 16)

            def rstd_group(g, tiles):
                pool.wait_ge(aggr_done, g + 1)
                own_wait(pool)
                nc.gpsimd.tensor_scalar(veA[:, 0:tiles], mvA[:, 0:tiles, 1], LN_EPS, None, ALU.add
                                        ).then_inc(eps_added, 1)
                pool.wait_ge(eps_added, g + 1)
                nc.gpsimd.tensor_tensor(rsA[:, 0:tiles], veA[:, 0:tiles], halfneg[:, 0:tiles], ALU.pow
                                        ).then_inc(rstd_ready, 1)

            with pool.Fori(0, NGRP) as g:
                rstd_group(g, GRP)
            rstd_group(NGRP, TXT_TILES)

            def norm_first(t, k, lap):
                s = stC[:, k, :]

                def link(m, ins):
                    ins.then_inc(norm_step, 1)
                    pool.wait_ge(norm_step, t * NORM + m)

                pool.wait_ge(first_step, t * FIRST + 2)
                own_wait(pool)
                link(1, nc.gpsimd.tensor_scalar(s[:, 0:1], mvC[:, 1:2], LN_EPS, None, ALU.add))
                link(2, nc.gpsimd.tensor_tensor(s[:, 1:2], s[:, 0:1], halfneg[:, 0:1], ALU.pow))
                link(3, nc.gpsimd.tensor_tensor(s[:, 2:3], mvC[:, 1:2], s[:, 1:2], ALU.mult))
                link(4, nc.gpsimd.tensor_tensor(s[:, 3:4], s[:, 2:3], s[:, 1:2], ALU.mult))
                own_wait(pool)
                link(5, nc.gpsimd.tensor_scalar(s[:, 4:5], s[:, 3:4], RMS_EPS, None, ALU.add))
                nc.gpsimd.tensor_tensor(s[:, 5:6], s[:, 4:5], halfneg[:, 0:1], ALU.pow).then_inc(norm_step, 1)

            def norm_second(t, k, lap):
                s = stC[:, k, :]
                pool.wait_ge(gelu_done, t + 2)
                pool.wait_ge(second_step, t * SECOND + 6)
                nc.gpsimd.tensor_tensor(uF[:], gl[:, k, :], g2b[:], ALU.mult).then_inc(scaled, 1)
                pool.wait_ge(second_step, t * SECOND + SECOND + 1)
                own_wait(pool)
                nc.gpsimd.tensor_scalar(s[:, 11:12], s[:, 10:11], 1.0 / DFF, RMS_EPS, ALU.mult, ALU.add
                                        ).then_inc(rms2_step, 1)
                pool.wait_ge(rms2_step, t * 2 + 1)
                nc.gpsimd.tensor_tensor(s[:, 12:13], s[:, 11:12], halfneg[:, 0:1], ALU.pow).then_inc(rms2_step, 1)

            stage_c(pool, norm_first, norm_second)

        @block.scalar
        def _(act):
            def group_a(g, tiles):
                cols = tiles * P
                act.wait_ge(zT_done, g + 2)
                act.wait_ge(v_done, g + 1)
                for a in range(2):
                    nc.scalar.copy(zT[0:DH, a, 0:cols], zTP[a][:, 0:cols]).then_inc(zT_copied, 1)
                act.wait_ge(qk_stored, g * (16 * 2 * NPART) + 16 * 2 * NPART)
                for which in range(2):
                    act.wait_ge(qk_done, g * 2 + which + 1)
                    nc.scalar.copy(split[:, which, 0, 0:cols], qkP[which][:, 0:cols]).then_inc(hi_ready, 1)
                act.wait_ge(v_done, g + 2)
                act.wait_ge(v_stored, g * 16 + 16)
                for t in range(tiles):
                    last = nc.scalar.copy(vA[:, :, t, 0:HD], vP[:, t, :].rearrange("p (h c) -> p h c", h=H))
                last.then_inc(v_copied, 1)

            act.wait_ge(weights_step, WEIGHT_STEPS)
            with act.Fori(0, NGRP) as g:
                group_a(g, GRP)
            group_a(NGRP, TXT_TILES)

            def exps(b, pair, par, following):
                seq = b * H + pair * 2 + par
                act.wait_ge(av_done, seq + 1)
                for n, (j, a, w) in enumerate(CHUNKS):
                    rows = P if j < NT else NTXT
                    act.wait_ge(s2_done, seq * NS2 + n + 1)
                    nc.scalar.activation(pT[0:rows, par, POFF[j] + a:POFF[j] + a + w], s2P[n % RING3][0:rows, 0:w],
                                         ACT.Exp).then_inc(exp_done, 1)

            def context_out(b):
                for t in range(NTT):
                    n = b * NTT + t
                    rows = P if t < NT else NTXT
                    act.wait_ge(cxT_done, n + 2)
                    act.wait_ge(proj_done, n + 1)
                    nc.scalar.copy(cxT[0:DC, t % RING3, 0:rows], cxTP[t % RING3][:, 0:rows]).then_inc(cxT_copied, 1)

            stage_b(act, lambda b: None, exps, context_out)

            def up_first(t, k, lap):
                act.wait_ge(x1T_done, t + 2)
                nc.scalar.copy(x1T[:], x1TP).then_inc(x1T_copied, 1)
                act.wait_ge(up_done, t + 1)
                act.wait_ge(first_step, t * FIRST + FIRST)
                nc.scalar.activation(gl[:, k, :].rearrange("p (a f) -> p a f", a=2), upP, ACT.Gelu,
                                     scale=stC[:, k, 13:14]).then_inc(gelu_done, 1)

            def down_second(t, k, lap):
                act.wait_ge(x2T_done, t + 2)
                nc.scalar.copy(x2T[:], x2TP).then_inc(x2T_copied, 1)

            stage_c(act, up_first, down_second)

        @block.vector
        def _(dve):
            count = [0]

            def link(ins):
                count[0] += 1
                ins.then_inc(weights_step, 1)
                dve.wait_ge(weights_step, count[0])

            for ap, value in ((ones[:], 1.0), (zT[DH:DH + 1, 1, :], 1.0), (vA[:, :, :, HD], 1.0), (cxT[DC:DC + 1], 1.0),
                              (qs[32:MROW], 0.0), (qs[MROW:96], 0.0), (ks[32:MROW], 0.0), (ks[MROW:96], 1.0),
                              (nmax[:], 0.0)):
                link(nc.vector.memset(ap, value))
            dve.wait_ge(setup_loaded, 16 * NSETUP)
            for t in range(NT):
                link(nc.vector.tensor_tensor(posb[:, t, :], posb[:, t, :], convb[:], ALU.add))
            link(nc.vector.tensor_reduce(wsum[0:DH, 0:1], w1f[:].rearrange("p a f -> p (a f)"), AX_X, ALU.add,
                                         apply_absolute_value=True))
            link(nc.vector.tensor_reduce(wsum[:, 1:2], w2f[:].rearrange("p a f -> p (a f)"), AX_X, ALU.add,
                                         apply_absolute_value=True))
            assert count[0] == SUM_STEPS
            dve.wait_ge(folded, 1)
            for m in range(3):
                factor = HD ** -0.5 if m == 0 else 1.0
                for a in range(2):
                    link(nc.vector.tensor_scalar(wqkv[0:DH + a, a, m, :], foldP[a][0:DH + a, m, :], factor, None, ALU.mult))
            link(nc.vector.tensor_copy(wout[0:DC, :], woutP))
            link(nc.vector.tensor_scalar(wscale[:], wsumP, 1.0 / (D * DFF), Q_EPS, ALU.mult, ALU.max))
            link(nc.vector.reciprocal(winv[:], wscale[:]))
            link(nc.vector.tensor_scalar(wdq[:], wscale[:], 1.0 / 127.0, None, ALU.mult))
            for n, (wf, wq, rows) in enumerate(((w1f, w1q, DH), (w2f, w2q, P))):
                link(nc.vector.tensor_scalar(wf[:], wf[:], winv[0:rows, n:n + 1], 1.0, ALU.mult, ALU.min))
                link(nc.vector.tensor_scalar(wf[:], wf[:], -1.0, MAGIC, ALU.max, ALU.add))
                link(nc.vector.tensor_scalar(wq[:], wf[:], MAGIC, None, ALU.subtract))
            assert count[0] == WEIGHT_STEPS

            def group_a(b, half, tiles, text):
                g = b * HALVES + half
                n0 = g * GRP
                for t in range(tiles):
                    if text:
                        if t == 0:
                            dve.wait_ge(gathered, 16 * TXT_TILES)
                            dve.wait_ge(h_stored[0], 16 * B + 16)
                        nc.vector.tensor_copy(hA[:, half, t, :], txt[:, t, :]).then_inc(h_ready, 1)
                    else:
                        if t == 0:
                            dve.wait_ge(h_stored[half], b * 16 + 16)
                        dve.wait_ge(conv_done, n0 + t + 1)
                        nc.vector.tensor_tensor(hA[:, half, t, :], convP[t % RING2], posb[:, half * GRP + t, :], ALU.add
                                                ).then_inc(h_ready, 1)
                for t in range(tiles):
                    dve.wait_ge(h_ready, n0 + t + 1 + RING2)
                    nc.vector.bn_stats(bnA[:, t, :], hA[:, half, t, :]).then_inc(stats_done, 1)
                for t in range(tiles):
                    dve.wait_ge(stats_done, n0 + t + 1)
                    own_wait(dve)
                    last = nc.vector.bn_aggr(mvA[:, t, :], bnA[:, t, :])
                last.then_inc(aggr_done, 1)
                dve.wait_ge(rstd_ready, g + 1)
                dve.wait_ge(zT_done, g + 1)
                for t in range(tiles):
                    nc.vector.tensor_scalar(zA[:, t, :], hA[:, half, t, :], mvA[:, t, 0:1], rsA[:, t:t + 1],
                                            ALU.subtract, ALU.mult).then_inc(z_ready, 1)
                cols = tiles * P
                for which in range(2):
                    hi, mid, lo = (split[:, which, part, 0:cols] for part in range(3))
                    n = g * 2 + which + 1
                    dve.wait_ge(hi_ready, n)
                    nc.vector.tensor_tensor(rest[:, which, 0:cols], qkP[which][:, 0:cols], hi, ALU.subtract
                                            ).then_inc(rest_ready, 1)
                    dve.wait_ge(rest_ready, n + 2)
                    nc.vector.tensor_copy(mid, rest[:, which, 0:cols]).then_inc(mid_ready, 1)
                    dve.wait_ge(mid_ready, n)
                    nc.vector.tensor_tensor(lo, rest[:, which, 0:cols], mid, ALU.subtract).then_inc(lo_ready, 1)

            with dve.Fori(0, B) as b:
                for half in range(HALVES):
                    group_a(b, half, GRP, False)
            group_a(B, 0, TXT_TILES, True)

            def maxima(seq):
                for u, (i, k0, w) in enumerate(S1_USES):
                    rows = P if i < NT else NTXT
                    col = i + (k0 > 0)
                    dve.wait_ge(s1_done, seq * NS1 + u + 1)
                    nc.vector.tensor_reduce(nmax[0:rows, col:col + 1], s1P[u % RING2][0:rows, 0:w], AX_X, ALU.max,
                                            negate=True).then_inc(s1_read, 1)
                dve.wait_ge(s1_read, seq * NS1 + len(S1_USES) + RING2)
                nc.vector.tensor_tensor(nmax[0:NTXT, NT:NTT], nmax[0:NTXT, NT:NTT], nmax[0:NTXT, NTT:NTT + 1], ALU.min
                                        ).then_inc(parts_step, 1)
                dve.wait_ge(parts_step, seq * 4 + 1)
                nc.vector.tensor_copy(nmparts[:, :, 0], nmax[:, 0:NTT]).then_inc(parts_step, 1)
                dve.wait_ge(parts_step, seq * 4 + 2)
                nc.vector.tensor_tensor(nmrest[:], nmax[:, 0:NTT], nmparts[:, :, 0], ALU.subtract).then_inc(parts_step, 1)
                dve.wait_ge(parts_step, seq * 4 + 3)
                nc.vector.tensor_copy(nmparts[:, :, 1], nmrest[:]).then_inc(parts_step, 1)
                dve.wait_ge(parts_step, seq * 4 + 4)
                nc.vector.tensor_tensor(nmparts[:, :, 2], nmrest[:], nmparts[:, :, 1], ALU.subtract
                                        ).then_inc(parts_ready, 1)

            def maxima_in(seq, par):
                dve.wait_ge(s1_done, seq * NS1 + NS1 - 1)
                nc.vector.tensor_copy(qs[MROW:KALL, par, 0:NPATCH], s1P[0][MROW:KALL, :]).then_inc(s1_read, 1)
                dve.wait_ge(s1_done, seq * NS1 + NS1)
                nc.vector.tensor_copy(qs[MROW:KALL, par, NPATCH:S], s1P[1][MROW:KALL, 0:NTXT]).then_inc(s1_read, 1)

            def head_step(b, pair, par, following):
                seq = b * H + pair * 2 + par
                if following:
                    maxima(seq + 1)
                av = avP
                dve.wait_ge(av_done, seq + 1 + RING2)
                nc.vector.reciprocal(rden[:, 0:NT], av[:, 0:NT, HD]).then_inc(rden_ready, 1)
                nc.vector.reciprocal(rden[0:NTXT, NT:NTT], av[0:NTXT, NT:NTT, HD]).then_inc(rden_ready, 1)
                dve.wait_ge(cxT_done, b * NTT + 1)
                dve.wait_ge(rden_ready, seq * 2 + 2)
                col = bass.ds((pair * 2 + par) * HD, HD)
                nc.vector.tensor_tensor(cx[:, 0:NT, col], av[:, 0:NT, 0:HD],
                                        rden[:, 0:NT].unsqueeze(2).to_broadcast([P, NT, HD]), ALU.mult)
                nc.vector.tensor_tensor(cx[0:NTXT, NT, col], av[0:NTXT, NT, 0:HD],
                                        rden[0:NTXT, NT:NTT].to_broadcast([NTXT, HD]), ALU.mult).then_inc(av_read, 1)
                if following:
                    maxima_in(seq + 1, 1 - par)

            def first_maxima(b):
                maxima(b * H)
                maxima_in(b * H, 0)

            def residual(b):
                dve.wait_ge(hB_loaded, b * 32 + 32)
                for t in range(NTT):
                    n = b * NTT + t
                    rows = P if t < NT else NTXT
                    dve.wait_ge(proj_done, n + 1 + RING3)
                    dve.wait_ge(h2_stored[t % RING3], (b * (NTT // RING3) + t // RING3) * 16 + 16)
                    nc.vector.tensor_tensor(h2B[0:rows, t % RING3, :], projP[t % RING3][0:rows], hB[0:rows, t, :], ALU.add
                                            ).then_inc(h2_ready, 1)

            stage_b(dve, first_maxima, head_step, residual)

            def quant_first(t, k, lap):
                s, h = stC[:, k, :], hC[:, k, :]
                base = t * FIRST

                def link(m, ins):
                    ins.then_inc(first_step, 1)
                    dve.wait_ge(first_step, base + m)

                dve.wait_ge(hC_loaded[k], lap * 16 + 16)
                link(1, nc.vector.bn_stats(bnC[:], h))
                own_wait(dve)
                nc.vector.bn_aggr(mvC[:], bnC[:]).then_inc(first_step, 1)
                dve.wait_ge(norm_step, t * NORM + 2)
                link(3, nc.vector.tensor_scalar(uC[:], h, mvC[:, 0:1], s[:, 1:2], ALU.subtract, ALU.mult))
                link(4, nc.vector.tensor_tensor(uC[:], uC[:], g1b[:], ALU.mult))
                link(5, nc.vector.tensor_reduce(s[:, 6:7], uC[:], AX_X, ALU.max, apply_absolute_value=True))
                dve.wait_ge(norm_step, t * NORM + NORM)
                link(6, nc.vector.tensor_scalar(s[:, 7:8], s[:, 6:7], s[:, 5:6], Q_EPS, ALU.mult, ALU.max))
                link(7, nc.vector.reciprocal(s[:, 8:9], s[:, 7:8]))
                link(8, nc.vector.scalar_tensor_tensor(out=s[:, 9:10], in0=s[:, 8:9], scalar=127.0, in1=s[:, 5:6],
                                                       op0=ALU.mult, op1=ALU.mult))
                link(9, nc.vector.tensor_scalar(tC[:], uC[:], s[:, 9:10], MAGIC, ALU.mult, ALU.add))
                dve.wait_ge(x1T_done, t + 1)
                nc.vector.tensor_scalar(xqC[:], tC[:], MAGIC, None, ALU.subtract).then_inc(first_step, 1)
                nc.vector.tensor_scalar(s[:, 13:14], s[:, 7:8], wdq[:, 0:1], None, ALU.mult).then_inc(first_step, 1)

            def quant_second(t, k, lap):
                s = stC[:, k, :]
                base = t * SECOND + SECOND

                def link(m, ins):
                    ins.then_inc(second_step, 1)
                    dve.wait_ge(second_step, base + m)

                dve.wait_ge(gelu_done, t + 2)
                nc.vector.tensor_tensor_reduce(out=sq[:], in0=gl[:, k, :], in1=gl[:, k, :], scale=1.0, scalar=0.0,
                                               op0=ALU.mult, op1=ALU.add, accum_out=s[:, 10:11]).then_inc(second_step, 1)
                dve.wait_ge(scaled, t + 1)
                link(2, nc.vector.tensor_reduce(s[:, 14:15], uF[:], AX_X, ALU.max, apply_absolute_value=True))
                dve.wait_ge(rms2_step, t * 2 + 2)
                link(3, nc.vector.tensor_scalar(s[:, 15:16], s[:, 14:15], s[:, 12:13], Q_EPS, ALU.mult, ALU.max))
                link(4, nc.vector.reciprocal(s[:, 8:9], s[:, 15:16]))
                link(5, nc.vector.scalar_tensor_tensor(out=s[:, 9:10], in0=s[:, 8:9], scalar=127.0, in1=s[:, 12:13],
                                                       op0=ALU.mult, op1=ALU.mult))
                link(6, nc.vector.tensor_scalar(tF[:], uF[:], s[:, 9:10], MAGIC, ALU.mult, ALU.add))
                dve.wait_ge(x2T_done, t + 1)
                nc.vector.tensor_scalar(xqF[:], tF[:], MAGIC, None, ALU.subtract).then_inc(second_step, 1)
                link(8, nc.vector.tensor_scalar(s[:, 13:14], s[:, 15:16], wdq[:, 1:2], None, ALU.mult))
                dve.wait_ge(down_done, t + 1)
                dve.wait_ge(out_stored[k], lap * 16 + 16)
                nc.vector.scalar_tensor_tensor(out=oC[:, k, :], in0=downP, scalar=s[:, 13:14], in1=hC[:, k, :],
                                               op0=ALU.mult, op1=ALU.add).then_inc(second_step, 1)

            stage_c(dve, quant_first, quant_second)

        @block.tensor
        def _(pe):
            mm = nc.tensor.matmul
            pe.wait_ge(setup_loaded, 16 * NSETUP)
            for a in range(2):
                for m in range(3):
                    for jj in range(2):
                        mm(foldP[a][0:DH + a, m, :], wat[:, 2 * m + jj, a * DH:a * DH + DH + a], pqkv[:, 2 * m + jj, :],
                           start=jj == 0, stop=jj == 1)
            for jj in range(2):
                mm(woutP, wbt[:, jj, :], wpj[:, jj, :], start=jj == 0, stop=jj == 1)
            pe.wait_ge(weights_step, SUM_STEPS)
            mm(wsumP[:, 0:1], ones[0:DH, :], wsum[0:DH, 0:1], start=True, stop=True)
            mm(wsumP[:, 1:2], ones[:], wsum[:, 1:2], start=True, stop=True).then_inc(folded, 1)
            pe.wait_ge(weights_step, WEIGHT_STEPS)
            pe.wait_ge(const_step, CONSTANTS)

            def group_a(g, half, lap, tiles):
                n0 = g * GRP
                if half is not None:
                    pe.wait_ge(x_loaded[half], lap * 16 + 16)
                    for t in range(tiles):
                        pe.wait_ge(h_ready, n0 + t + 1)
                        for k in range(KT):
                            last = mm(convP[t % RING2], xt[:, half, k, t * P:t * P + P], convw[:, k, :],
                                      start=k == 0, stop=k == KT - 1)
                        last.then_inc(conv_done, 1)
                pe.wait_ge(zT_copied, g * 2 + 2)
                for t in range(tiles):
                    pe.wait_ge(z_ready, n0 + t + 1)
                    for a in range(2):
                        last = nc.tensor.transpose(zTP[a][:, t * P:t * P + P], zA[:, t, a * DH:a * DH + DH], identf[:])
                last.then_inc(zT_done, 1)
                cols = tiles * P
                pe.wait_ge(zT_copied, g * 2 + 4)
                for which in range(2):
                    pe.wait_ge(rest_ready, g * 2 + which + 1)
                    for a in range(2):
                        last = mm(qkP[which][:, 0:cols], wqkv[0:DH + a, a, which, :], zT[0:DH + a, a, 0:cols],
                                  start=a == 0, stop=a == 1)
                    last.then_inc(qk_done, 1)
                pe.wait_ge(v_copied, g + 1)
                for t in range(tiles):
                    for a in range(2):
                        last = mm(vP[:, t, :], zT[0:DH + a, a, t * P:t * P + P], wqkv[0:DH + a, a, 2, :],
                                  start=a == 0, stop=a == 1)
                last.then_inc(v_done, 1)

            with pe.Fori(0, B) as b:
                for half in range(HALVES):
                    group_a(b * HALVES + half, half, b, GRP)
            group_a(NGRP, None, None, TXT_TILES)

            def row_scores(seq, par, u):
                i, k0, w = S1_USES[u]
                rows = P if i < NT else NTXT
                place = s1P[u % RING2]
                pe.wait_ge(s1_read, seq * NS1 + u + 1)
                if rows < P:
                    own_wait(pe)
                diag = P * i - k0 if i < NT or k0 else None
                for c in range(0, w, 512):
                    cw = min(512, w - c)
                    last = mm(place[0:rows, c:c + cw], qs[0:KROWS, par, P * i:P * i + rows],
                              ks[0:KROWS, par, k0 + c:k0 + c + cw], start=True, stop=True, skip_group_check=True)
                    if diag is not None and c <= diag < c + cw:
                        last = mm(place[0:rows, diag:diag + rows], tri[0:rows, 0:rows], ident[0:rows, 0:rows],
                                  start=False, stop=True, skip_group_check=True)
                last.then_inc(s1_done, 1)

            def maxima_as_rows(seq):
                pe.wait_ge(parts_ready, seq + 1)
                pe.wait_ge(s1_read, seq * NS1 + NS1 - 1)
                for t in range(NT):
                    last = mm(s1P[0][MROW:KALL, P * t:P * t + P], nmparts[:, t, :], ident[:], start=True, stop=True)
                last.then_inc(s1_done, 1)
                pe.wait_ge(s1_read, seq * NS1 + NS1)
                own_wait(pe)
                mm(s1P[1][MROW:KALL, 0:NTXT], nmparts[0:NTXT, NT, :], ident[0:NTXT, 0:NTXT], start=True, stop=True
                   ).then_inc(s1_done, 1)

            def row_pass(seq, par):
                for u in range(len(S1_USES)):
                    row_scores(seq, par, u)
                maxima_as_rows(seq)

            def first_maxima(b):
                pe.wait_ge(qkv_loaded[0], b * (64 * (H // 2)) + 64)
                row_pass(b * H, 0)

            def head_step(b, pair, par, following):
                seq = b * H + pair * 2 + par

                def times_v(j):
                    pe.wait_ge(exp_done, seq * NS2 + DONE_AT[j] + RING3)
                    keys = P if j < NT else NTXT
                    if keys < P:
                        own_wait(pe)
                    for i in range(j, NTT):
                        rows = P if i < NT else NTXT
                        col = POFF[j] + P * (i - j)
                        last = mm(avP[0:rows, i, :], pT[0:keys, par, col:col + rows], vs[0:keys, par, j, :],
                                  start=(j == 0 and i == 0), stop=(i == j), skip_group_check=True)
                    if j == NT:
                        last.then_inc(av_done, 1)

                pe.wait_ge(s1_read, seq * NS1 + NS1 + RING2)
                if following:
                    lap = b * (H // 2) + pair + par
                    pe.wait_ge(qkv_loaded[1 - par], lap * 64 + 64)
                pe.wait_ge(av_read, seq + 1)
                n = 0
                for j in range(NTT):
                    keys = P if j < NT else NTXT
                    for a, w in s2_chunks(j):
                        place = s2P[n % RING3]
                        pe.wait_ge(exp_done, seq * NS2 + n + 1)
                        if keys < P:
                            own_wait(pe)
                        last = mm(place[0:keys, 0:w], ks[0:KALL, par, P * j:P * j + keys],
                                  qs[0:KALL, par, P * j + a:P * j + a + w], start=True, stop=True, skip_group_check=True)
                        if a == 0:
                            last = mm(place[0:keys, 0:keys], ident[0:keys, 0:keys], tri[0:keys, 0:keys],
                                      start=False, stop=True, skip_group_check=True)
                        last.then_inc(s2_done, 1)
                        n += 1
                    if following:
                        row_scores(seq + 1, 1 - par, j)
                        if j == NT:
                            row_scores(seq + 1, 1 - par, j + 1)
                    if j:
                        times_v(j - 1)
                times_v(NT)
                if following:
                    maxima_as_rows(seq + 1)

            def project(b):
                pe.wait_ge(av_read, b * H + H + 1)
                for t in range(NTT):
                    n = b * NTT + t
                    rows = P if t < NT else NTXT
                    pe.wait_ge(cxT_copied, n + 1)
                    if rows < P:
                        own_wait(pe)
                    nc.tensor.transpose(cxTP[t % RING3][:, 0:rows], cx[0:rows, t, :], identf[0:rows, 0:rows]
                                        ).then_inc(cxT_done, 1)
                    pe.wait_ge(h2_ready, n + 1)
                    pe.wait_ge(cxT_copied, n + 1 + RING3)
                    mm(projP[t % RING3][0:rows], cxT[:, t % RING3, 0:rows], wout[:], start=True, stop=True
                       ).then_inc(proj_done, 1)
                pe.wait_ge(h2_ready, b * NTT + NTT + RING3)

            stage_b(pe, first_maxima, head_step, project)

            def up_first(t, k, lap):
                pe.wait_ge(first_step, t * FIRST + FIRST - 1)
                pe.wait_ge(x1T_copied, t + 1)
                for a in range(2):
                    last = nc.tensor.transpose(x1TP[:, a, :], xqC[:, a * DH:a * DH + DH], ident[:])
                last.then_inc(x1T_done, 1)
                pe.wait_ge(gelu_done, t + 1)
                pe.wait_ge(x1T_copied, t + 2)
                for half in range(2):
                    for a in range(2):
                        last = mm(upP[:, half, :], x1T[:, a, :], w1q[:, a, half * UPW:half * UPW + UPW],
                                  start=a == 0, stop=a == 1)
                last.then_inc(up_done, 1)

            def down_second(t, k, lap):
                pe.wait_ge(second_step, t * SECOND + SECOND + 7)
                pe.wait_ge(x2T_copied, t + 1)
                for f in range(FT):
                    last = nc.tensor.transpose(x2TP[:, f, :], xqF[:, f * P:f * P + P], ident[:])
                last.then_inc(x2T_done, 1)
                pe.wait_ge(x2T_copied, t + 2)
                for f in range(FT):
                    last = mm(downP, x2T[:, f, :], w2q[:, f, :], start=f == 0, stop=f == FT - 1)
                last.then_inc(down_done, 1)

            stage_c(pe, up_first, down_second)


def kernel(**inputs):
    import numpy as np
    import concourse.bacc as bacc
    from concourse.bass_utils import run_bass_kernel_spmd

    a = {name: np.asarray(value) for name, value in inputs.items()}

    def tiles(x, rows):
        return np.ascontiguousarray(x.reshape(x.shape[0] // rows, rows, -1).transpose(1, 0, 2))

    side = SIDE * PATCH
    patches = a["x"][:, :, :side, :side].reshape(B, C_IN, SIDE, PATCH, SIDE, PATCH)
    patches = patches.transpose(1, 3, 5, 0, 2, 4).reshape(KT, P, NGRP, W)
    pos_ids = patch_positions()
    arrays = {
        "xT": np.ascontiguousarray(patches.transpose(2, 1, 0, 3)),
        "idx": np.ascontiguousarray(a["x_txt"].reshape(TXT_TILES, P).T),
        "conv_w": tiles(a["L0_tok_conv_w"].reshape(D, KC).T, P),
        "conv_b": a["L0_tok_conv_b"],
        "pos": tiles(a["L0_tok_pos_table"][pos_ids], P),
        "emb": np.ascontiguousarray(a["L0_txt_weight"].T),
        "w_attn": tiles(np.concatenate([a["L0_attn_W_attn"].T, a["L0_attn_b_attn"][:, None]], axis=1), DH),
        "p_q": tiles(a["L0_attn_P_q"], DH),
        "p_k": tiles(a["L0_attn_P_k"], DH),
        "p_v": tiles(a["L0_attn_P_v"], DH),
        "w_back": tiles(a["L0_attn_W_back"].T, DH),
        "w_proj": tiles(a["L0_attn_W_proj"], DH),
        "b_proj": a["L0_attn_b_proj"].reshape(1, D),
        "w1": tiles(a["L0_ffn_w1"].T, DH),
        "g1": a["L0_ffn_g1"],
        "w2": tiles(a["L0_ffn_w2"].T, P),
        "g2": a["L0_ffn_g2"],
    }
    nc = bacc.Bacc("TRN2", target_bir_lowering=False, num_devices=1)
    args = [nc.dram_tensor(f"in_{name}", x.shape, mybir.dt.from_np(x.dtype), kind="ExternalInput").ap()
            for name, x in arrays.items()]
    args.append(nc.dram_tensor("out_tokens", (TOK, D), F32, kind="ExternalOutput").ap())
    early_fusion_kernel(nc, *args)
    r = run_bass_kernel_spmd(nc, [{f"in_{name}": x for name, x in arrays.items()}], core_ids=[0])
    return r.results[0]["out_tokens"].reshape(B, S, D)


def patch_positions():
    import numpy as np

    boundaries = np.arange(1.0 / SIDE, 1.0, 1.0 / SIDE, dtype=np.float32)
    frac = np.arange(0.0, 1.0 - 1e-06, 1.0 / SIDE, dtype=np.float32)
    at = np.searchsorted(boundaries, frac, side="right")
    return (at[:, None] * SIDE + at).reshape(-1)
```

```python
from contextlib import ExitStack

import concourse.bass as bass
from concourse import mybir

F32 = mybir.dt.float32
BF16 = mybir.dt.bfloat16
I32 = mybir.dt.int32
ALU = mybir.AluOpType
ACT = mybir.ActivationFunctionType
AX_X = mybir.AxisListType.X

P = 128
B, C_IN, IMG, PATCH = 8, 3, 518, 16
SIDE = IMG // PATCH
NPATCH = SIDE * SIDE
NTXT = 32
S = NPATCH + NTXT
D, DC, H = 192, 96, 12
HD = DC // H
DH = D // 2
DFF = 768
KC = C_IN * PATCH * PATCH
KT = KC // P
NT = NPATCH // P
NTT = NT + 1
GRP = 4
W = GRP * P
HALVES = NT // GRP
NGRP = B * HALVES
TXT_TILES = B * NTXT // P
NPART = 6
KROWS = NPART * HD
MROW = 64
KALL = MROW + 3
VW = HD + 1
TOK = B * S
CT = TOK // P
FT = DFF // P
UPW = DFF // 2
NEG = -1.0e30
MAGIC = 1.5 * 2.0 ** 23
LN_EPS, RMS_EPS, Q_EPS = 1e-5, 1e-6, 1e-5
PARTS_Q = (0, 1, 2, 0, 1, 0)
PARTS_K = (0, 0, 0, 1, 1, 2)


def s2_chunks(j):
    left = S - P * j
    n = -(-left // 512)
    w = -(-left // (n * 32)) * 32
    return [(c * w, min(w, left - c * w)) for c in range(n)]


ORDER = range(NT, -1, -1)
CHUNKS = [(j, a, w) for j in ORDER for a, w in s2_chunks(j)]
NS2 = len(CHUNKS)
DONE_AT = [max(n for n, c in enumerate(CHUNKS) if c[0] == j) + 1 for j in range(NTT)]
POFF = [sum(S - P * i for i in range(j)) for j in range(NTT)]
PCOLS = POFF[NT] + NTXT
S1_USES = [(i, 0, P * (i + 1)) for i in range(NT)] + [(NT, 0, NPATCH), (NT, NPATCH, NTXT)]
NS1 = len(S1_USES)
S1_AT = [2, 1, 1, 1, 1, 1, 1, 2]
RUNS = [(0, 512), (512, 512), (NPATCH, NTXT)]
CR = H * VW
RING2, RING3 = 2, 3
CONSTANTS = 7
NSETUP = 16
SUM_STEPS = 9 + NT + 2
WEIGHT_STEPS = SUM_STEPS + 16
FIRST, SECOND = 11, 9
NORM = 6


def early_fusion_kernel(nc, xT, idx, conv_w, conv_b, pos, emb, w_attn, p_q, p_k, p_v, w_back, w_proj, b_proj,
                        sum_rows, row_of_ones, w1, g1, w2, g2, out):
    q_dram = nc.dram_tensor("q_stacked", (B, DC, NPART, S), BF16, kind="Internal").ap()
    k_dram = nc.dram_tensor("k_stacked", (B, DC, NPART, S), BF16, kind="Internal").ap()
    v_dram = nc.dram_tensor("v_tiles", (B, H, P, NTT, VW), F32, kind="Internal").ap()
    c_dram = nc.dram_tensor("context", (B, CR, S), F32, kind="Internal").ap()
    h_dram = nc.dram_tensor("embedded", (B, S, D), F32, kind="Internal").ap()
    h2_dram = nc.dram_tensor("attended", (TOK, D), F32, kind="Internal").ap()

    with ExitStack() as ctx:
        def sb(name, shape, dt=F32):
            return ctx.enter_context(nc.sbuf_tensor(name, shape, dt))

        def sem(name):
            return ctx.enter_context(nc.semaphore(name))

        psum = ctx.enter_context(nc.psum_tensor("psum", [P, 8, 512], F32))

        identf = sb("identf", [P, P])
        ident = sb("ident", [P, P], BF16)
        tri = sb("tri", [P, P], BF16)
        ones = sb("ones", [P, P])
        halfneg = sb("halfneg", [P, GRP])
        idx_sb = sb("idx_sb", [P, TXT_TILES], I32)
        txt = sb("txt", [P, TXT_TILES, D])
        convw = sb("convw", [P, KT, D])
        posb = sb("posb", [P, NT, D])
        convb = sb("convb", [P, D])
        wat = sb("wat", [DH, 6, D + 1])
        pqkv = sb("pqkv", [DH, 6, DC])
        wqkv = sb("wqkv", [DH + 1, 2, 3, DC])
        wbt = sb("wbt", [DH, 2, CR])
        wpj = sb("wpj", [DH, 2, D])
        wout = sb("wout", [CR + 1, D])
        w1f = sb("w1f", [DH, 2, DFF])
        w2f = sb("w2f", [P, FT, D])
        w1q = sb("w1q", [DH, 2, DFF], BF16)
        w2q = sb("w2q", [P, FT, D], BF16)
        g1b = sb("g1b", [P, D])
        g2b = sb("g2b", [P, DFF])
        wsum = sb("wsum", [P, 2])
        wscale = sb("wscale", [P, 2])
        winv = sb("winv", [P, 2])
        wdq = sb("wdq", [P, 2])

        xt = sb("xt", [P, RING2, KT, W])
        hA = sb("hA", [P, RING2, GRP, D])
        bnA = sb("bnA", [P, GRP, 6])
        mvA = sb("mvA", [P, GRP, 2])
        veA = sb("veA", [P, GRP])
        rsA = sb("rsA", [P, GRP])
        zA = sb("zA", [P, GRP, D])
        zT = sb("zT", [DH + 1, 2, W])
        split = sb("split", [DC, 2, 3, W], BF16)
        rest = sb("rest", [DC, 2, W])
        vA = sb("vA", [P, H, GRP, VW])

        qs = sb("qs", [P, RING2, S], BF16)
        ks = sb("ks", [P, RING2, S], BF16)
        vs = sb("vs", [P, RING2, NTT, VW])
        pT = sb("pT", [P, RING2, PCOLS])
        nmax = sb("nmax", [P, NTT + 1])
        nmrest = sb("nmrest", [P, NTT])
        nmparts = sb("nmparts", [P, NTT, 3], BF16)
        av = sb("av", [96, RING2, 512])
        cx = sb("cx", [CR, S])
        sumrow = sb("sumrow", [CR, CR])
        rden = sb("rden", [CR, S])
        cxn = sb("cxn", [CR + 1, S])
        hB = sb("hB", [P, NTT, D])
        h2B = sb("h2B", [P, RING3, D])

        hC = sb("hC", [P, RING3, D])
        bnC = sb("bnC", [P, 6])
        mvC = sb("mvC", [P, 2])
        stC = sb("stC", [P, RING3, 16])
        uC = sb("uC", [P, D])
        tC = sb("tC", [P, D])
        xqC = sb("xqC", [P, D], BF16)
        x1T = sb("x1T", [DH, 2, P], BF16)
        gl = sb("gl", [P, RING3, DFF])
        sq = sb("sq", [P, DFF])
        uF = sb("uF", [P, DFF])
        tF = sb("tF", [P, DFF])
        xqF = sb("xqF", [P, DFF], BF16)
        x2T = sb("x2T", [P, FT, P], BF16)
        oC = sb("oC", [P, RING3, D])

        idx_loaded, gathered = sem("idx_loaded"), sem("gathered")
        setup_loaded = sem("setup_loaded")
        const_step = sem("const_step")
        weights_step = sem("weights_step")
        folded = sem("folded")
        x_loaded = [sem("x_loaded0"), sem("x_loaded1")]
        conv_done, h_ready = sem("conv_done"), sem("h_ready")
        stats_done, aggr_done = sem("stats_done"), sem("aggr_done")
        eps_added, rstd_ready = sem("eps_added"), sem("rstd_ready")
        z_ready, zT_done, zT_copied = sem("z_ready"), sem("zT_done"), sem("zT_copied")
        qk_done, v_done = sem("qk_done"), sem("v_done")
        hi_ready, rest_ready = sem("hi_ready"), sem("rest_ready")
        mid_ready, lo_ready = sem("mid_ready"), sem("lo_ready")
        v_copied = sem("v_copied")
        h_stored = [sem("h_stored0"), sem("h_stored1")]
        qk_stored, v_stored = sem("qk_stored"), sem("v_stored")
        qkv_loaded = [sem("qkv_loaded0"), sem("qkv_loaded1")]
        hB_loaded = sem("hB_loaded")
        s1_done, s1_read = sem("s1_done"), sem("s1_read")
        parts_step, parts_ready = sem("parts_step"), sem("parts_ready")
        s2_done, exp_done = sem("s2_done"), sem("exp_done")
        maxT_done, maxT_in = sem("maxT_done"), sem("maxT_in")
        av_done, av_read = sem("av_done"), sem("av_read")
        cx_placed = [sem("cx_placed0"), sem("cx_placed1")]
        cx_loaded = sem("cx_loaded")
        sums_done, rden_ready, cxn_ready = sem("sums_done"), sem("rden_ready"), sem("cxn_ready")
        proj_done, h2_ready = sem("proj_done"), sem("h2_ready")
        h2_stored = [sem(f"h2_stored{i}") for i in range(RING3)]
        hC_loaded = [sem(f"hC_loaded{i}") for i in range(RING3)]
        first_step = sem("first_step")
        second_step = sem("second_step")
        norm_step = sem("norm_step")
        scaled, rms2_step = sem("scaled"), sem("rms2_step")
        x1T_done, x1T_copied, up_done, gelu_done = sem("x1T_done"), sem("x1T_copied"), sem("up_done"), sem("gelu_done")
        x2T_done, x2T_copied, down_done = sem("x2T_done"), sem("x2T_copied"), sem("down_done")
        out_stored = [sem(f"out_stored{i}") for i in range(RING3)]
        waits_met = sem("waits_met")

        block = ctx.enter_context(nc.Block())

        def own_wait(eng):
            eng.sem_inc(waits_met, 1)

        def stage_c(eng, first, second):
            first(0, 0, 0)
            with eng.Fori(0, CT // RING3 - 1) as i:
                for k in range(RING3):
                    first(i * RING3 + k + 1, (k + 1) % RING3, i + (k + 1) // RING3)
                    second(i * RING3 + k, k, i)
            for t in range(CT - RING3, CT):
                if t < CT - 1:
                    first(t + 1, (t + 1) % RING3, (t + 1) // RING3)
                second(t, t % RING3, t // RING3)

        def stage_b(eng, before, head_step, after):
            with eng.Fori(0, B) as b:
                before(b)
                with eng.Fori(0, H // 2 - 1) as pair:
                    for par in range(RING2):
                        head_step(b, pair, par, True)
                head_step(b, H // 2 - 1, 0, True)
                head_step(b, H // 2 - 1, 1, False)
                after(b)

        convP = [psum[:, i, 0:D] for i in range(RING2)]
        zTP = [psum[0:DH, 2 + a, :] for a in range(2)]
        qkP = [psum[0:DC, 4 + i, :] for i in range(2)]
        vP = psum[:, 6, 0:GRP * DC].rearrange("p (t c) -> p t c", t=GRP)
        s1P = [psum[:, 2 * i:2 * i + 2, :].rearrange("p a b -> p (a b)") for i in range(RING2)]
        s2P = [psum[:, 4 + i, :] for i in range(RING3)]
        avP = psum[0:96, 7, :]
        sumsP = [psum[0:CR, 4 + i, 0:S // 3] for i in range(RING3)]
        projP = [psum[:, i, 0:D] for i in range(RING3)]
        x1TP = psum[0:DH, 0, 0:P].bitcast(BF16).rearrange("p (a t) -> p a t", a=2)
        upP = psum[:, 1:3, 0:UPW]
        x2TP = psum[:, 3, 0:FT * P // 2].bitcast(BF16).rearrange("p (f t) -> p f t", f=FT)
        downP = psum[:, 4, 0:D]
        foldP = [psum[0:DH + 1, a, 0:3 * DC].rearrange("p (m c) -> p m c", m=3) for a in range(2)]
        woutP = psum[0:CR, 2, 0:D]
        wsumP = psum[:, 3, 0:2]

        @block.sync
        def _(sp):
            sp.dma_start(idx_sb[:], idx).then_inc(idx_loaded, 16)
            sp.dma_start(wat[:], w_attn).then_inc(setup_loaded, 16)
            sp.dma_start(pqkv[:, 0:2, :], p_q).then_inc(setup_loaded, 16)
            sp.dma_start(pqkv[:, 2:4, :], p_k).then_inc(setup_loaded, 16)
            sp.dma_start(pqkv[:, 4:6, :], p_v).then_inc(setup_loaded, 16)
            sp.dma_start(convw[:], conv_w).then_inc(setup_loaded, 16)
            sp.dma_start(xt[:, 0], xT[0]).then_inc(x_loaded[0], 16)
            sp.dma_start(posb[:], pos).then_inc(setup_loaded, 16)
            sp.dma_start(convb[:], conv_b.partition_broadcast(P)).then_inc(setup_loaded, 16)
            sp.dma_start(g1b[:], g1.partition_broadcast(P)).then_inc(setup_loaded, 16)
            sp.dma_start(g2b[:], g2.partition_broadcast(P)).then_inc(setup_loaded, 16)
            sp.dma_start(wbt[:], w_back).then_inc(setup_loaded, 16)
            sp.dma_start(wpj[:], w_proj).then_inc(setup_loaded, 16)
            sp.dma_start(wout[CR:CR + 1, :], b_proj).then_inc(setup_loaded, 16)
            sp.dma_start(sumrow[:], sum_rows).then_inc(setup_loaded, 16)
            sp.dma_start(cxn[CR:CR + 1, :], row_of_ones).then_inc(setup_loaded, 16)
            sp.dma_start(w1f[:], w1).then_inc(setup_loaded, 16)
            sp.dma_start(w2f[:], w2).then_inc(setup_loaded, 16)
            sp.dma_start(xt[:, 1], xT[1]).then_inc(x_loaded[1], 16)

            def store_group(g, b, half, tiles):
                lo, hi = half * W, half * W + W
                if b is None:
                    sp.wait_ge(h_ready, RING2 + NGRP * GRP + tiles)
                    for t in range(tiles):
                        for bb in range(GRP):
                            sp.dma_start(h_dram[GRP * t + bb, NPATCH:S, :],
                                         hA[NTXT * bb:NTXT * bb + NTXT, 0, t, :]).then_inc(h_stored[0], 16)
                else:
                    sp.wait_ge(h_ready, g * GRP + RING2 + tiles)
                    sp.dma_start(h_dram[bass.ds(b, 1), lo:hi, :].rearrange("a (t p) d -> (a p) t d", p=P),
                                 hA[:, half]).then_inc(h_stored[half], 16)
                sp.wait_ge(hi_ready, g * 2 + 2)
                sp.wait_ge(mid_ready, g * 2 + 2)
                sp.wait_ge(lo_ready, g * 2 + 2)
                for which, dram, parts in ((0, q_dram, PARTS_Q), (1, k_dram, PARTS_K)):
                    for slot in range(NPART):
                        src = split[:, which, parts[slot], :]
                        if b is None:
                            sp.dma_start(dram[:, :, slot, NPATCH:S].rearrange("b p t -> p b t"),
                                         src[:, 0:B * NTXT].rearrange("p (b t) -> p b t", b=B)).then_inc(qk_stored, 16)
                        else:
                            sp.dma_start(dram[bass.ds(b, 1), :, slot, lo:hi].rearrange("a p t -> (a p) t"),
                                         src).then_inc(qk_stored, 16)
                sp.wait_ge(v_copied, g + 2)
                if b is None:
                    for t in range(tiles):
                        for bb in range(GRP):
                            sp.dma_start(v_dram[GRP * t + bb, :, 0:NTXT, NT, :].rearrange("h p c -> p h c"),
                                         vA[NTXT * bb:NTXT * bb + NTXT, :, t, :]).then_inc(v_stored, 16)
                else:
                    sp.dma_start(v_dram[bass.ds(b, 1), :, :, half * GRP:half * GRP + GRP, :]
                                 .rearrange("a h p t c -> (a p) h (t c)"),
                                 vA[:].rearrange("p h t c -> p h (t c)")).then_inc(v_stored, 16)

            def batch_stores(b, prefetch):
                for half in range(HALVES):
                    g = b * HALVES + half
                    if prefetch:
                        sp.wait_ge(conv_done, g * GRP + GRP)
                        sp.dma_start(xt[:, half], xT[bass.ds(g + RING2, 1)].rearrange("a p k t -> (a p) k t")
                                     ).then_inc(x_loaded[half], 16)
                    store_group(g, b, half, GRP)

            with sp.Fori(0, B - 1) as b:
                batch_stores(b, True)
            batch_stores(B - 1, False)
            store_group(NGRP, None, 0, TXT_TILES)

            sp.wait_ge(h_stored[0], 16 * (1 + B + B))
            sp.wait_ge(h_stored[1], 16 * (1 + B))
            sp.wait_ge(qk_stored, 16 * 2 * NPART * (1 + NGRP + 1))
            sp.wait_ge(v_stored, 16 * (1 + NGRP + B))

            with sp.Fori(0, B) as b:
                sp.wait_ge(h2_ready, b * NTT + RING3)
                sp.dma_start(hB[:, 0:NT, :], h_dram[bass.ds(b, 1), 0:NPATCH, :].rearrange("a (t p) d -> (a p) t d", p=P)
                             ).then_inc(hB_loaded, 16)
                sp.dma_start(hB[0:NTXT, NT, :], h_dram[bass.ds(b, 1), NPATCH:S, :].rearrange("a t d -> (a t) d")
                             ).then_inc(hB_loaded, 16)

                def load_head(head, par):
                    sp.wait_ge(av_done, b * H + head + 1)
                    for ring, dram in ((qs, q_dram), (ks, k_dram)):
                        sp.dma_start(ring[0:KROWS, par, :],
                                     dram[bass.ds(b, 1), bass.ds(head * HD, HD)].rearrange("a r s t -> (a r s) t")
                                     ).then_inc(qkv_loaded[par], 16)
                    sp.dma_start(vs[:, par, 0:NT, :],
                                 v_dram[bass.ds(b, 1), bass.ds(head, 1), :, 0:NT, :]
                                 .rearrange("a h p t c -> (a h p) t c")).then_inc(qkv_loaded[par], 16)
                    sp.dma_start(vs[0:NTXT, par, NT, :],
                                 v_dram[bass.ds(b, 1), bass.ds(head, 1), 0:NTXT, NT, :]
                                 .rearrange("a h p c -> (a h p) c")).then_inc(qkv_loaded[par], 16)

                def place_context(head, par):
                    sp.wait_ge(av_read, b * H + head + 2)
                    for r, (q0, w) in enumerate(RUNS):
                        sp.dma_start(c_dram[bass.ds(b, 1), bass.ds(head * VW, VW), q0:q0 + w].rearrange("a r t -> (a r) t"),
                                     av[32 * r:32 * r + VW, par, 0:w]).then_inc(cx_placed[par], 16)

                load_head(0, 0)
                load_head(1, 1)
                with sp.Fori(0, H // 2 - 1) as pair:
                    for par in range(2):
                        load_head(pair * 2 + par + 2, par)
                        place_context(pair * 2 + par, par)
                place_context(H - 2, 0)
                place_context(H - 1, 1)
                for par in range(2):
                    sp.wait_ge(cx_placed[par], b * (48 * (H // 2)) + 48 * (H // 2) + 48)
                own_wait(sp)
                sp.dma_start(cx[:], c_dram[bass.ds(b, 1)].rearrange("a r t -> (a r) t")).then_inc(cx_loaded, 16)
                for t in range(NTT):
                    rows = P if t < NT else NTXT
                    sp.wait_ge(h2_ready, b * NTT + t + 1 + RING3)
                    sp.dma_start(h2_dram[bass.ds(b * S + t * P, rows), :],
                                 h2B[0:rows, t % RING3, :]).then_inc(h2_stored[t % RING3], 16)

            for k in range(RING3):
                sp.wait_ge(h2_stored[k], 16 * (1 + B * NTT // RING3))

            def load_tile(row, k):
                sp.dma_start(hC[:, k, :], h2_dram[row, :]).then_inc(hC_loaded[k], 16)

            for k in range(RING3):
                load_tile(slice(P * k, P * k + P), k)
            with sp.Fori(0, CT // RING3 - 1) as i:
                for k in range(RING3):
                    t = i * RING3 + k
                    sp.wait_ge(second_step, t * SECOND + 2 * SECOND)
                    sp.dma_start(out[bass.ds(t * P, P), :], oC[:, k, :]).then_inc(out_stored[k], 16)
                    load_tile(bass.ds((t + RING3) * P, P), k)
            for k in range(RING3):
                t = CT - RING3 + k
                sp.wait_ge(second_step, t * SECOND + 2 * SECOND)
                sp.dma_start(out[t * P:t * P + P, :], oC[:, k, :]).then_inc(out_stored[k], 16)
            for k in range(RING3):
                sp.wait_ge(out_stored[k], 16 * (1 + CT // RING3))

        @block.gpsimd
        def _(pool):
            for s, n in ((h_ready, RING2), (h_stored[0], 16), (h_stored[1], 16), (zT_done, 1), (zT_copied, 2), (v_done, 1),
                         (rest_ready, 2), (v_copied, 1), (qk_stored, 16 * 2 * NPART), (v_stored, 16),
                         (av_done, RING2), (s1_read, RING2), (maxT_in, 2), (exp_done, RING3), (av_read, 1), (cx_placed[0], 48), (cx_placed[1], 48),
                         (sums_done, 3), (rden_ready, 3), (cxn_ready, 3), (proj_done, NTT), (h2_ready, RING3), *((q, 16) for q in h2_stored),
                         *((q, 16) for q in out_stored), (x1T_done, 1), (x1T_copied, 1), (gelu_done, 1), (x2T_done, 1),
                         (x2T_copied, 1), (second_step, SECOND)):
                pool.sem_inc(s, n)
            nc.gpsimd.memset(ident[:], 0.0).then_inc(const_step, 1)
            nc.gpsimd.memset(identf[:], 0.0).then_inc(const_step, 1)
            nc.gpsimd.memset(tri[:], 0.0).then_inc(const_step, 1)
            nc.gpsimd.memset(halfneg[:], -0.5).then_inc(const_step, 1)
            pool.wait_ge(const_step, 4)
            nc.gpsimd.affine_select(out=ident[:], in_=ident[:], compare_op=ALU.not_equal, fill=1.0, base=0,
                                    pattern=[[-1, P]], channel_multiplier=1).then_inc(const_step, 1)
            nc.gpsimd.affine_select(out=identf[:], in_=identf[:], compare_op=ALU.not_equal, fill=1.0, base=0,
                                    pattern=[[-1, P]], channel_multiplier=1).then_inc(const_step, 1)
            nc.gpsimd.affine_select(out=tri[:], in_=tri[:], compare_op=ALU.is_ge, fill=NEG, base=0,
                                    pattern=[[1, P]], channel_multiplier=-1).then_inc(const_step, 1)
            pool.wait_ge(idx_loaded, 16)
            for t in range(TXT_TILES):
                nc.gpsimd.indirect_dma_start(out=txt[:, t, :], out_offset=None, in_=emb,
                                             in_offset=bass.IndirectOffsetOnAxis(ap=idx_sb[:, t:t + 1], axis=0)
                                             ).then_inc(gathered, 16)

            def rstd_group(g, tiles):
                pool.wait_ge(aggr_done, g + 1)
                own_wait(pool)
                nc.gpsimd.tensor_scalar(veA[:, 0:tiles], mvA[:, 0:tiles, 1], LN_EPS, None, ALU.add
                                        ).then_inc(eps_added, 1)
                pool.wait_ge(eps_added, g + 1)
                nc.gpsimd.tensor_tensor(rsA[:, 0:tiles], veA[:, 0:tiles], halfneg[:, 0:tiles], ALU.pow
                                        ).then_inc(rstd_ready, 1)

            with pool.Fori(0, NGRP) as g:
                rstd_group(g, GRP)
            rstd_group(NGRP, TXT_TILES)

            def norm_first(t, k, lap):
                s = stC[:, k, :]

                def link(m, ins):
                    ins.then_inc(norm_step, 1)
                    pool.wait_ge(norm_step, t * NORM + m)

                pool.wait_ge(first_step, t * FIRST + 2)
                own_wait(pool)
                link(1, nc.gpsimd.tensor_scalar(s[:, 0:1], mvC[:, 1:2], LN_EPS, None, ALU.add))
                link(2, nc.gpsimd.tensor_tensor(s[:, 1:2], s[:, 0:1], halfneg[:, 0:1], ALU.pow))
                link(3, nc.gpsimd.tensor_tensor(s[:, 2:3], mvC[:, 1:2], s[:, 1:2], ALU.mult))
                link(4, nc.gpsimd.tensor_tensor(s[:, 3:4], s[:, 2:3], s[:, 1:2], ALU.mult))
                own_wait(pool)
                link(5, nc.gpsimd.tensor_scalar(s[:, 4:5], s[:, 3:4], RMS_EPS, None, ALU.add))
                nc.gpsimd.tensor_tensor(s[:, 5:6], s[:, 4:5], halfneg[:, 0:1], ALU.pow).then_inc(norm_step, 1)

            def norm_second(t, k, lap):
                s = stC[:, k, :]
                pool.wait_ge(gelu_done, t + 2)
                pool.wait_ge(second_step, t * SECOND + 6)
                nc.gpsimd.tensor_tensor(uF[:], gl[:, k, :], g2b[:], ALU.mult).then_inc(scaled, 1)
                pool.wait_ge(second_step, t * SECOND + SECOND + 1)
                own_wait(pool)
                nc.gpsimd.tensor_scalar(s[:, 11:12], s[:, 10:11], 1.0 / DFF, RMS_EPS, ALU.mult, ALU.add
                                        ).then_inc(rms2_step, 1)
                pool.wait_ge(rms2_step, t * 2 + 1)
                nc.gpsimd.tensor_tensor(s[:, 12:13], s[:, 11:12], halfneg[:, 0:1], ALU.pow).then_inc(rms2_step, 1)

            stage_c(pool, norm_first, norm_second)

        @block.scalar
        def _(act):
            def group_a(g, tiles):
                cols = tiles * P
                act.wait_ge(zT_done, g + 2)
                act.wait_ge(v_done, g + 1)
                for a in range(2):
                    nc.scalar.copy(zT[0:DH, a, 0:cols], zTP[a][:, 0:cols]).then_inc(zT_copied, 1)
                act.wait_ge(qk_stored, g * (16 * 2 * NPART) + 16 * 2 * NPART)
                for which in range(2):
                    act.wait_ge(qk_done, g * 2 + which + 1)
                    nc.scalar.copy(split[:, which, 0, 0:cols], qkP[which][:, 0:cols]).then_inc(hi_ready, 1)
                act.wait_ge(v_done, g + 2)
                act.wait_ge(v_stored, g * 16 + 16)
                for t in range(tiles):
                    last = nc.scalar.copy(vA[:, :, t, 0:HD], vP[:, t, :].rearrange("p (h c) -> p h c", h=H))
                last.then_inc(v_copied, 1)

            act.wait_ge(weights_step, WEIGHT_STEPS)
            with act.Fori(0, NGRP) as g:
                group_a(g, GRP)
            group_a(NGRP, TXT_TILES)

            def maxima_in(seq, par):
                act.wait_ge(maxT_done, seq * 2 + 1)
                nc.scalar.copy(qs[MROW:KALL, par, 0:NPATCH], s1P[0][MROW:KALL, :]).then_inc(maxT_in, 1)
                act.wait_ge(maxT_done, seq * 2 + 2)
                nc.scalar.copy(qs[MROW:KALL, par, NPATCH:S], s1P[1][MROW:KALL, 0:NTXT]).then_inc(maxT_in, 1)

            def exps(b, pair, par, following):
                seq = b * H + pair * 2 + par
                act.wait_ge(av_done, seq + 1)
                for n, (j, a, w) in enumerate(CHUNKS):
                    rows = P if j < NT else NTXT
                    act.wait_ge(s2_done, seq * NS2 + n + 1)
                    nc.scalar.activation(pT[0:rows, par, POFF[j] + a:POFF[j] + a + w], s2P[n % RING3][0:rows, 0:w],
                                         ACT.Exp).then_inc(exp_done, 1)
                if following:
                    maxima_in(seq + 1, 1 - par)
                act.wait_ge(av_done, seq + 1 + RING2)
                act.wait_ge(cx_placed[par], (b * (H // 2) + pair) * 48 + 48)
                nc.scalar.copy(av[:, par, :], avP).then_inc(av_read, 1)

            act.wait_ge(weights_step, WEIGHT_STEPS)
            stage_b(act, lambda b: maxima_in(b * H, 0), exps, lambda b: None)

            def up_first(t, k, lap):
                act.wait_ge(x1T_done, t + 2)
                nc.scalar.copy(x1T[:], x1TP).then_inc(x1T_copied, 1)
                act.wait_ge(up_done, t + 1)
                act.wait_ge(first_step, t * FIRST + FIRST)
                nc.scalar.activation(gl[:, k, :].rearrange("p (a f) -> p a f", a=2), upP, ACT.Gelu,
                                     scale=stC[:, k, 13:14]).then_inc(gelu_done, 1)

            def down_second(t, k, lap):
                act.wait_ge(x2T_done, t + 2)
                nc.scalar.copy(x2T[:], x2TP).then_inc(x2T_copied, 1)

            stage_c(act, up_first, down_second)

        @block.vector
        def _(dve):
            count = [0]

            def link(ins):
                count[0] += 1
                ins.then_inc(weights_step, 1)
                dve.wait_ge(weights_step, count[0])

            for ap, value in ((ones[:], 1.0), (zT[DH:DH + 1, 1, :], 1.0), (vA[:, :, :, HD], 1.0), (psum[:, 7, :], 0.0),
                              (qs[32:MROW], 0.0), (qs[MROW:96], 0.0), (ks[32:MROW], 0.0), (ks[MROW:96], 1.0),
                              (nmax[:], 0.0)):
                link(nc.vector.memset(ap, value))
            dve.wait_ge(setup_loaded, 16 * NSETUP)
            for t in range(NT):
                link(nc.vector.tensor_tensor(posb[:, t, :], posb[:, t, :], convb[:], ALU.add))
            link(nc.vector.tensor_reduce(wsum[0:DH, 0:1], w1f[:].rearrange("p a f -> p (a f)"), AX_X, ALU.add,
                                         apply_absolute_value=True))
            link(nc.vector.tensor_reduce(wsum[:, 1:2], w2f[:].rearrange("p a f -> p (a f)"), AX_X, ALU.add,
                                         apply_absolute_value=True))
            assert count[0] == SUM_STEPS
            dve.wait_ge(folded, 1)
            for m in range(3):
                factor = HD ** -0.5 if m == 0 else 1.0
                for a in range(2):
                    link(nc.vector.tensor_scalar(wqkv[0:DH + a, a, m, :], foldP[a][0:DH + a, m, :], factor, None, ALU.mult))
            link(nc.vector.tensor_copy(wout[0:CR, :], woutP))
            link(nc.vector.tensor_scalar(wscale[:], wsumP, 1.0 / (D * DFF), Q_EPS, ALU.mult, ALU.max))
            link(nc.vector.reciprocal(winv[:], wscale[:]))
            link(nc.vector.tensor_scalar(wdq[:], wscale[:], 1.0 / 127.0, None, ALU.mult))
            for n, (wf, wq, rows) in enumerate(((w1f, w1q, DH), (w2f, w2q, P))):
                link(nc.vector.tensor_scalar(wf[:], wf[:], winv[0:rows, n:n + 1], 1.0, ALU.mult, ALU.min))
                link(nc.vector.tensor_scalar(wf[:], wf[:], -1.0, MAGIC, ALU.max, ALU.add))
                link(nc.vector.tensor_scalar(wq[:], wf[:], MAGIC, None, ALU.subtract))
            assert count[0] == WEIGHT_STEPS

            def group_a(b, half, tiles, text):
                g = b * HALVES + half
                n0 = g * GRP
                for t in range(tiles):
                    if text:
                        if t == 0:
                            dve.wait_ge(gathered, 16 * TXT_TILES)
                            dve.wait_ge(h_stored[0], 16 * B + 16)
                        nc.vector.tensor_copy(hA[:, half, t, :], txt[:, t, :]).then_inc(h_ready, 1)
                    else:
                        if t == 0:
                            dve.wait_ge(h_stored[half], b * 16 + 16)
                        dve.wait_ge(conv_done, n0 + t + 1)
                        nc.vector.tensor_tensor(hA[:, half, t, :], convP[t % RING2], posb[:, half * GRP + t, :], ALU.add
                                                ).then_inc(h_ready, 1)
                for t in range(tiles):
                    dve.wait_ge(h_ready, n0 + t + 1 + RING2)
                    nc.vector.bn_stats(bnA[:, t, :], hA[:, half, t, :]).then_inc(stats_done, 1)
                for t in range(tiles):
                    dve.wait_ge(stats_done, n0 + t + 1)
                    own_wait(dve)
                    last = nc.vector.bn_aggr(mvA[:, t, :], bnA[:, t, :])
                last.then_inc(aggr_done, 1)
                dve.wait_ge(rstd_ready, g + 1)
                dve.wait_ge(zT_done, g + 1)
                for t in range(tiles):
                    nc.vector.tensor_scalar(zA[:, t, :], hA[:, half, t, :], mvA[:, t, 0:1], rsA[:, t:t + 1],
                                            ALU.subtract, ALU.mult).then_inc(z_ready, 1)
                cols = tiles * P
                for which in range(2):
                    hi, mid, lo = (split[:, which, part, 0:cols] for part in range(3))
                    n = g * 2 + which + 1
                    dve.wait_ge(hi_ready, n)
                    nc.vector.tensor_tensor(rest[:, which, 0:cols], qkP[which][:, 0:cols], hi, ALU.subtract
                                            ).then_inc(rest_ready, 1)
                    dve.wait_ge(rest_ready, n + 2)
                    nc.vector.tensor_copy(mid, rest[:, which, 0:cols]).then_inc(mid_ready, 1)
                    dve.wait_ge(mid_ready, n)
                    nc.vector.tensor_tensor(lo, rest[:, which, 0:cols], mid, ALU.subtract).then_inc(lo_ready, 1)

            with dve.Fori(0, B) as b:
                for half in range(HALVES):
                    group_a(b, half, GRP, False)
            group_a(B, 0, TXT_TILES, True)

            def maxima(seq):
                for u, (i, k0, w) in enumerate(S1_USES):
                    rows = P if i < NT else NTXT
                    col = i + (k0 > 0)
                    dve.wait_ge(s1_done, seq * NS1 + u + 1)
                    nc.vector.tensor_reduce(nmax[0:rows, col:col + 1], s1P[u % RING2][0:rows, 0:w], AX_X, ALU.max,
                                            negate=True).then_inc(s1_read, 1)
                dve.wait_ge(s1_read, seq * NS1 + NS1 + RING2)
                nc.vector.tensor_tensor(nmax[0:NTXT, NT:NTT], nmax[0:NTXT, NT:NTT], nmax[0:NTXT, NTT:NTT + 1], ALU.min
                                        ).then_inc(parts_step, 1)
                dve.wait_ge(parts_step, seq * 4 + 1)
                nc.vector.tensor_copy(nmparts[:, :, 0], nmax[:, 0:NTT]).then_inc(parts_step, 1)
                dve.wait_ge(parts_step, seq * 4 + 2)
                nc.vector.tensor_tensor(nmrest[:], nmax[:, 0:NTT], nmparts[:, :, 0], ALU.subtract).then_inc(parts_step, 1)
                dve.wait_ge(parts_step, seq * 4 + 3)
                nc.vector.tensor_copy(nmparts[:, :, 1], nmrest[:]).then_inc(parts_step, 1)
                dve.wait_ge(parts_step, seq * 4 + 4)
                nc.vector.tensor_tensor(nmparts[:, :, 2], nmrest[:], nmparts[:, :, 1], ALU.subtract
                                        ).then_inc(parts_ready, 1)

            def next_maxima(b, pair, par, following):
                if following:
                    maxima(b * H + pair * 2 + par + 1)

            def normalise(b):
                for c in range(3):
                    n = b * 3 + c
                    cols = slice(c * (S // 3), (c + 1) * (S // 3))
                    dve.wait_ge(sums_done, n + 1 + 3)
                    nc.vector.reciprocal(rden[:, cols], sumsP[c]).then_inc(rden_ready, 1)
                    dve.wait_ge(rden_ready, n + 1 + 3)
                    if c == 0:
                        dve.wait_ge(proj_done, b * NTT + NTT)
                    nc.vector.tensor_tensor(cxn[0:CR, cols], cx[:, cols], rden[:, cols], ALU.mult
                                            ).then_inc(cxn_ready, 1)
                dve.wait_ge(hB_loaded, b * 32 + 32)
                for t in range(NTT):
                    n = b * NTT + t
                    rows = P if t < NT else NTXT
                    dve.wait_ge(proj_done, n + 1 + NTT)
                    dve.wait_ge(h2_stored[t % RING3], (b * (NTT // RING3) + t // RING3) * 16 + 16)
                    nc.vector.tensor_tensor(h2B[0:rows, t % RING3, :], projP[t % RING3][0:rows], hB[0:rows, t, :], ALU.add
                                            ).then_inc(h2_ready, 1)

            stage_b(dve, lambda b: maxima(b * H), next_maxima, normalise)

            def quant_first(t, k, lap):
                s, h = stC[:, k, :], hC[:, k, :]
                base = t * FIRST

                def link(m, ins):
                    ins.then_inc(first_step, 1)
                    dve.wait_ge(first_step, base + m)

                dve.wait_ge(hC_loaded[k], lap * 16 + 16)
                link(1, nc.vector.bn_stats(bnC[:], h))
                own_wait(dve)
                nc.vector.bn_aggr(mvC[:], bnC[:]).then_inc(first_step, 1)
                dve.wait_ge(norm_step, t * NORM + 2)
                link(3, nc.vector.tensor_scalar(uC[:], h, mvC[:, 0:1], s[:, 1:2], ALU.subtract, ALU.mult))
                link(4, nc.vector.tensor_tensor(uC[:], uC[:], g1b[:], ALU.mult))
                link(5, nc.vector.tensor_reduce(s[:, 6:7], uC[:], AX_X, ALU.max, apply_absolute_value=True))
                dve.wait_ge(norm_step, t * NORM + NORM)
                link(6, nc.vector.tensor_scalar(s[:, 7:8], s[:, 6:7], s[:, 5:6], Q_EPS, ALU.mult, ALU.max))
                link(7, nc.vector.reciprocal(s[:, 8:9], s[:, 7:8]))
                link(8, nc.vector.scalar_tensor_tensor(out=s[:, 9:10], in0=s[:, 8:9], scalar=127.0, in1=s[:, 5:6],
                                                       op0=ALU.mult, op1=ALU.mult))
                link(9, nc.vector.tensor_scalar(tC[:], uC[:], s[:, 9:10], MAGIC, ALU.mult, ALU.add))
                dve.wait_ge(x1T_done, t + 1)
                nc.vector.tensor_scalar(xqC[:], tC[:], MAGIC, None, ALU.subtract).then_inc(first_step, 1)
                nc.vector.tensor_scalar(s[:, 13:14], s[:, 7:8], wdq[:, 0:1], None, ALU.mult).then_inc(first_step, 1)

            def quant_second(t, k, lap):
                s = stC[:, k, :]
                base = t * SECOND + SECOND

                def link(m, ins):
                    ins.then_inc(second_step, 1)
                    dve.wait_ge(second_step, base + m)

                dve.wait_ge(gelu_done, t + 2)
                nc.vector.tensor_tensor_reduce(out=sq[:], in0=gl[:, k, :], in1=gl[:, k, :], scale=1.0, scalar=0.0,
                                               op0=ALU.mult, op1=ALU.add, accum_out=s[:, 10:11]).then_inc(second_step, 1)
                dve.wait_ge(scaled, t + 1)
                link(2, nc.vector.tensor_reduce(s[:, 14:15], uF[:], AX_X, ALU.max, apply_absolute_value=True))
                dve.wait_ge(rms2_step, t * 2 + 2)
                link(3, nc.vector.tensor_scalar(s[:, 15:16], s[:, 14:15], s[:, 12:13], Q_EPS, ALU.mult, ALU.max))
                link(4, nc.vector.reciprocal(s[:, 8:9], s[:, 15:16]))
                link(5, nc.vector.scalar_tensor_tensor(out=s[:, 9:10], in0=s[:, 8:9], scalar=127.0, in1=s[:, 12:13],
                                                       op0=ALU.mult, op1=ALU.mult))
                link(6, nc.vector.tensor_scalar(tF[:], uF[:], s[:, 9:10], MAGIC, ALU.mult, ALU.add))
                dve.wait_ge(x2T_done, t + 1)
                nc.vector.tensor_scalar(xqF[:], tF[:], MAGIC, None, ALU.subtract).then_inc(second_step, 1)
                link(8, nc.vector.tensor_scalar(s[:, 13:14], s[:, 15:16], wdq[:, 1:2], None, ALU.mult))
                dve.wait_ge(down_done, t + 1)
                dve.wait_ge(out_stored[k], lap * 16 + 16)
                nc.vector.scalar_tensor_tensor(out=oC[:, k, :], in0=downP, scalar=s[:, 13:14], in1=hC[:, k, :],
                                               op0=ALU.mult, op1=ALU.add).then_inc(second_step, 1)

            stage_c(dve, quant_first, quant_second)

        @block.tensor
        def _(pe):
            mm = nc.tensor.matmul
            pe.wait_ge(setup_loaded, 16 * NSETUP)
            for a in range(2):
                for m in range(3):
                    for jj in range(2):
                        mm(foldP[a][0:DH + a, m, :], wat[:, 2 * m + jj, a * DH:a * DH + DH + a], pqkv[:, 2 * m + jj, :],
                           start=jj == 0, stop=jj == 1)
            for jj in range(2):
                mm(woutP, wbt[:, jj, :], wpj[:, jj, :], start=jj == 0, stop=jj == 1)
            pe.wait_ge(weights_step, SUM_STEPS)
            mm(wsumP[:, 0:1], ones[0:DH, :], wsum[0:DH, 0:1], start=True, stop=True)
            mm(wsumP[:, 1:2], ones[:], wsum[:, 1:2], start=True, stop=True).then_inc(folded, 1)
            pe.wait_ge(weights_step, WEIGHT_STEPS)
            pe.wait_ge(const_step, CONSTANTS)

            def group_a(g, half, lap, tiles):
                n0 = g * GRP
                if half is not None:
                    pe.wait_ge(x_loaded[half], lap * 16 + 16)
                    for t in range(tiles):
                        pe.wait_ge(h_ready, n0 + t + 1)
                        for k in range(KT):
                            last = mm(convP[t % RING2], xt[:, half, k, t * P:t * P + P], convw[:, k, :],
                                      start=k == 0, stop=k == KT - 1)
                        last.then_inc(conv_done, 1)
                pe.wait_ge(zT_copied, g * 2 + 2)
                for t in range(tiles):
                    pe.wait_ge(z_ready, n0 + t + 1)
                    for a in range(2):
                        last = nc.tensor.transpose(zTP[a][:, t * P:t * P + P], zA[:, t, a * DH:a * DH + DH], identf[:])
                last.then_inc(zT_done, 1)
                cols = tiles * P
                pe.wait_ge(zT_copied, g * 2 + 4)
                for which in range(2):
                    pe.wait_ge(rest_ready, g * 2 + which + 1)
                    for a in range(2):
                        last = mm(qkP[which][:, 0:cols], wqkv[0:DH + a, a, which, :], zT[0:DH + a, a, 0:cols],
                                  start=a == 0, stop=a == 1)
                    last.then_inc(qk_done, 1)
                pe.wait_ge(v_copied, g + 1)
                for t in range(tiles):
                    for a in range(2):
                        last = mm(vP[:, t, :], zT[0:DH + a, a, t * P:t * P + P], wqkv[0:DH + a, a, 2, :],
                                  start=a == 0, stop=a == 1)
                last.then_inc(v_done, 1)

            with pe.Fori(0, B) as b:
                for half in range(HALVES):
                    group_a(b * HALVES + half, half, b, GRP)
            group_a(NGRP, None, None, TXT_TILES)

            def row_scores(seq, par, u):
                i, k0, w = S1_USES[u]
                rows = P if i < NT else NTXT
                place = s1P[u % RING2]
                pe.wait_ge(s1_read, seq * NS1 + u + 1)
                if u < RING2:
                    pe.wait_ge(maxT_in, seq * 2 + u + 1)
                if rows < P:
                    own_wait(pe)
                diag = P * i - k0 if i < NT or k0 else None
                for c in range(0, w, 512):
                    cw = min(512, w - c)
                    last = mm(place[0:rows, c:c + cw], qs[0:KROWS, par, P * i:P * i + rows],
                              ks[0:KROWS, par, k0 + c:k0 + c + cw], start=True, stop=True, skip_group_check=True)
                    if diag is not None and c <= diag < c + cw:
                        last = mm(place[0:rows, diag:diag + rows], tri[0:rows, 0:rows], ident[0:rows, 0:rows],
                                  start=False, stop=True, skip_group_check=True)
                last.then_inc(s1_done, 1)

            def maxima_as_rows(seq):
                pe.wait_ge(parts_ready, seq + 1)
                for t in range(NT):
                    last = mm(s1P[0][MROW:KALL, P * t:P * t + P], nmparts[:, t, :], ident[:], start=True, stop=True)
                last.then_inc(maxT_done, 1)
                mm(s1P[1][MROW:KALL, 0:NTXT], nmparts[0:NTXT, NT, :], ident[0:NTXT, 0:NTXT], start=True, stop=True
                   ).then_inc(maxT_done, 1)

            def first_maxima(b):
                pe.wait_ge(qkv_loaded[0], b * (64 * (H // 2)) + 64)
                for u in range(NS1):
                    row_scores(b * H, 0, u)
                maxima_as_rows(b * H)

            def head_step(b, pair, par, following):
                seq = b * H + pair * 2 + par
                started = [False] * len(RUNS)

                def times_v(j):
                    pe.wait_ge(exp_done, seq * NS2 + DONE_AT[j] + RING3)
                    keys = P if j < NT else NTXT
                    if j == NT:
                        pe.wait_ge(av_read, seq + 1)
                        own_wait(pe)
                    for r, (q0, w) in enumerate(RUNS):
                        lo = max(P * j, q0)
                        if lo >= q0 + w:
                            continue
                        col = POFF[j] + lo - P * j
                        last = mm(avP[32 * r:32 * r + VW, lo - q0:w], vs[0:keys, par, j, :],
                                  pT[0:keys, par, col:col + q0 + w - lo], start=not started[r], stop=True,
                                  skip_group_check=True)
                        started[r] = True
                    return last

                pe.wait_ge(maxT_in, seq * 2 + 2 + 2)
                if following:
                    lap = b * (H // 2) + pair + par
                    pe.wait_ge(qkv_loaded[1 - par], lap * 64 + 64)
                n, u = 0, 0
                for step_n, j in enumerate(ORDER):
                    keys = P if j < NT else NTXT
                    for a, w in s2_chunks(j):
                        place = s2P[n % RING3]
                        pe.wait_ge(exp_done, seq * NS2 + n + 1)
                        if keys < P:
                            own_wait(pe)
                        last = mm(place[0:keys, 0:w], ks[0:KALL, par, P * j:P * j + keys],
                                  qs[0:KALL, par, P * j + a:P * j + a + w], start=True, stop=True, skip_group_check=True)
                        if a == 0:
                            last = mm(place[0:keys, 0:keys], ident[0:keys, 0:keys], tri[0:keys, 0:keys],
                                      start=False, stop=True, skip_group_check=True)
                        last.then_inc(s2_done, 1)
                        n += 1
                    if following and step_n < len(S1_AT):
                        for _ in range(S1_AT[step_n]):
                            row_scores(seq + 1, 1 - par, u)
                            u += 1
                    if step_n:
                        times_v(ORDER[step_n - 1])
                if following:
                    maxima_as_rows(seq + 1)
                times_v(0).then_inc(av_done, 1)

            def project(b):
                pe.wait_ge(cx_loaded, b * 16 + 16)
                for c in range(3):
                    n = b * 3 + c
                    pe.wait_ge(rden_ready, n + 1)
                    mm(sumsP[c], sumrow[:], cx[:, c * (S // 3):(c + 1) * (S // 3)], start=True, stop=True
                       ).then_inc(sums_done, 1)
                pe.wait_ge(cxn_ready, b * 3 + 3 + 3)
                for t in range(NTT):
                    n = b * NTT + t
                    rows = P if t < NT else NTXT
                    pe.wait_ge(h2_ready, n + 1)
                    mm(projP[t % RING3][0:rows], cxn[:, P * t:P * t + rows], wout[:], start=True, stop=True
                       ).then_inc(proj_done, 1)
                pe.wait_ge(h2_ready, b * NTT + NTT + RING3)

            stage_b(pe, first_maxima, head_step, project)

            def up_first(t, k, lap):
                pe.wait_ge(first_step, t * FIRST + FIRST - 1)
                pe.wait_ge(x1T_copied, t + 1)
                for a in range(2):
                    last = nc.tensor.transpose(x1TP[:, a, :], xqC[:, a * DH:a * DH + DH], ident[:])
                last.then_inc(x1T_done, 1)
                pe.wait_ge(gelu_done, t + 1)
                pe.wait_ge(x1T_copied, t + 2)
                for half in range(2):
                    for a in range(2):
                        last = mm(upP[:, half, :], x1T[:, a, :], w1q[:, a, half * UPW:half * UPW + UPW],
                                  start=a == 0, stop=a == 1)
                last.then_inc(up_done, 1)

            def down_second(t, k, lap):
                pe.wait_ge(second_step, t * SECOND + SECOND + 7)
                pe.wait_ge(x2T_copied, t + 1)
                for f in range(FT):
                    last = nc.tensor.transpose(x2TP[:, f, :], xqF[:, f * P:f * P + P], ident[:])
                last.then_inc(x2T_done, 1)
                pe.wait_ge(x2T_copied, t + 2)
                for f in range(FT):
                    last = mm(downP, x2T[:, f, :], w2q[:, f, :], start=f == 0, stop=f == FT - 1)
                last.then_inc(down_done, 1)

            stage_c(pe, up_first, down_second)


def kernel(**inputs):
    import numpy as np
    import concourse.bacc as bacc
    from concourse.bass_utils import run_bass_kernel_spmd

    a = {name: np.asarray(value) for name, value in inputs.items()}

    def tiles(x, rows):
        return np.ascontiguousarray(x.reshape(x.shape[0] // rows, rows, -1).transpose(1, 0, 2))

    side = SIDE * PATCH
    patches = a["x"][:, :, :side, :side].reshape(B, C_IN, SIDE, PATCH, SIDE, PATCH)
    patches = patches.transpose(1, 3, 5, 0, 2, 4).reshape(KT, P, NGRP, W)
    pos_ids = patch_positions()
    w_back = np.zeros((D, H, VW), np.float32)
    w_back[:, :, 0:HD] = a["L0_attn_W_back"].T.reshape(D, H, HD)
    sum_rows = np.zeros((H, VW, H, VW), np.float32)
    for h in range(H):
        sum_rows[h, HD, h, :] = 1.0
    sum_rows = sum_rows.reshape(CR, CR)
    arrays = {
        "xT": np.ascontiguousarray(patches.transpose(2, 1, 0, 3)),
        "idx": np.ascontiguousarray(a["x_txt"].reshape(TXT_TILES, P).T),
        "conv_w": tiles(a["L0_tok_conv_w"].reshape(D, KC).T, P),
        "conv_b": a["L0_tok_conv_b"],
        "pos": tiles(a["L0_tok_pos_table"][pos_ids], P),
        "emb": np.ascontiguousarray(a["L0_txt_weight"].T),
        "w_attn": tiles(np.concatenate([a["L0_attn_W_attn"].T, a["L0_attn_b_attn"][:, None]], axis=1), DH),
        "p_q": tiles(a["L0_attn_P_q"], DH),
        "p_k": tiles(a["L0_attn_P_k"], DH),
        "p_v": tiles(a["L0_attn_P_v"], DH),
        "w_back": tiles(w_back.reshape(D, CR), DH),
        "w_proj": tiles(a["L0_attn_W_proj"], DH),
        "b_proj": a["L0_attn_b_proj"].reshape(1, D),
        "sum_rows": sum_rows,
        "row_of_ones": np.ones((1, S), np.float32),
        "w1": tiles(a["L0_ffn_w1"].T, DH),
        "g1": a["L0_ffn_g1"],
        "w2": tiles(a["L0_ffn_w2"].T, P),
        "g2": a["L0_ffn_g2"],
    }
    nc = bacc.Bacc("TRN2", target_bir_lowering=False, num_devices=1)
    args = [nc.dram_tensor(f"in_{name}", x.shape, mybir.dt.from_np(x.dtype), kind="ExternalInput").ap()
            for name, x in arrays.items()]
    args.append(nc.dram_tensor("out_tokens", (TOK, D), F32, kind="ExternalOutput").ap())
    early_fusion_kernel(nc, *args)
    r = run_bass_kernel_spmd(nc, [{f"in_{name}": x for name, x in arrays.items()}], core_ids=[0])
    return r.results[0]["out_tokens"].reshape(B, S, D)


def patch_positions():
    import numpy as np

    boundaries = np.arange(1.0 / SIDE, 1.0, 1.0 / SIDE, dtype=np.float32)
    frac = np.arange(0.0, 1.0 - 1e-06, 1.0 / SIDE, dtype=np.float32)
    at = np.searchsorted(boundaries, frac, side="right")
    return (at[:, None] * SIDE + at).reshape(-1)
```

```python
from contextlib import ExitStack

import concourse.bass as bass
import numpy as np
from concourse import mybir

F32 = mybir.dt.float32
BF16 = mybir.dt.bfloat16
F16 = mybir.dt.float16
I32 = mybir.dt.int32
ALU = mybir.AluOpType
ACT = mybir.ActivationFunctionType
AX_X = mybir.AxisListType.X

P = 128
B, C_IN, IMG, PATCH = 8, 3, 518, 16
SIDE = IMG // PATCH
NPATCH = SIDE * SIDE
NTXT = 32
S = NPATCH + NTXT
D, DC, H = 192, 96, 12
HD = DC // H
DH = D // 2
DFF = 768
KC = C_IN * PATCH * PATCH
KT = KC // P
NT = NPATCH // P
NTT = NT + 1
GRP = 4
W = GRP * P
HALVES = NT // GRP
NGRP = B * HALVES
TXT_TILES = B * NTXT // P
NPART = 6
KROWS = NPART * HD
MROW = 96
KALL = MROW + 4
EXP_SHIFT = 10.375
VW = HD + 1
VP = 3
TOK = B * S
CT = TOK // P
FT = DFF // P
UPW = DFF // 2
NEG = -1.0e30
MAGIC = 1.5 * 2.0 ** 23
LN_EPS, RMS_EPS, Q_EPS = 1e-5, 1e-6, 1e-5
PARTS_Q = (0, 1, 2, 0, 1, 0)
PARTS_K = (0, 0, 0, 1, 1, 2)


def s2_chunks(j):
    left = S - P * j
    n = -(-left // 512)
    w = -(-left // (n * 32)) * 32
    return [(c * w, min(w, left - c * w)) for c in range(n)]


ORDER = range(NT, -1, -1)
CHUNKS = [(j, a, w) for j in ORDER for a, w in s2_chunks(j)]
NS2 = len(CHUNKS)
DONE_AT = [max(n for n, c in enumerate(CHUNKS) if c[0] == j) + 1 for j in range(NTT)]
POFF = [sum(S - P * i for i in range(j)) for j in range(NTT)]
PCOLS = POFF[NT] + NTXT
S1_USES = [(i, 0, P * (i + 1)) for i in range(NT)] + [(NT, 0, NPATCH), (NT, NPATCH, NTXT)]
NS1 = len(S1_USES)
S1_AFTER = {1: (0, 1), 2: (2,), 3: (3, 4), 5: (5,), 7: (6,), 8: (7,), 10: (8, 9)}
BEHIND_AFTER = {1: (1,), 3: (0,)}
AV_AFTER = {7: (8, 7), 8: (6, 5), 9: (4,), 12: (3,), 14: (2,)}
AV_OUT_AT = 3
MAXIMA_IN_AT = 13
RUNS = [(0, 512), (512, 512), (NPATCH, NTXT)]
POOL_CHUNKS = [n for n in range(NS2) if n % 2 == 0 and 0 < n < NS2 - 1]
DVE_CHUNKS = [n for n in range(NS2) if n not in POOL_CHUNKS]


def low_counts(n):
    back = 0 if n >= 0 else 1
    last = n + back * NS2
    return [sum(c <= last for c in chunks) - back * len(chunks) for chunks in (DVE_CHUNKS, POOL_CHUNKS)]


HEADS = B * H
CR = H * VW
RING2, RING3, RING5 = 2, 3, 5
SHARED = RING2 * KT * W + RING5 * 512 + PCOLS + RING2 * VP * S
CONSTANTS = 7
FILLED = CONSTANTS + 6
FOLD_LOADS, EMBED_LOADS, LATE_LOADS = 6, 3, 6
FOLD_STEPS = 7 + NT + 7
SUM_STEPS = FOLD_STEPS + 2
WEIGHT_STEPS = SUM_STEPS + 9
CGRP = 3
CG = CT // CGRP
TWO_PLACES = (0, 1, 0)
SINCE = (1, 3, 2)
NORM, QUANT = 7, 5


def early_fusion_kernel(nc, xT, idx, conv_w, conv_b, pos, emb, w_attn, p_q, p_k, p_v, w_back, w_proj, b_proj,
                        spread_rows, row_of_ones, w1, g1, w2, g2, out):
    q_dram = nc.dram_tensor("q_stacked", (B * DC, NPART, S), BF16, kind="Internal").ap()
    k_dram = nc.dram_tensor("k_stacked", (B * DC, NPART, S), BF16, kind="Internal").ap()
    v_dram = nc.dram_tensor("v_tiles", (B, H, P, NTT, VW, VP), BF16, kind="Internal").ap()
    c_dram = nc.dram_tensor("context", (HEADS, VW * VP, S), F32, kind="Internal").ap()
    h_dram = nc.dram_tensor("embedded", (B, S, D), F32, kind="Internal").ap()
    h2_dram = nc.dram_tensor("attended", (TOK, D), F32, kind="Internal").ap()

    with ExitStack() as ctx:
        def sb(name, shape, dt=F32):
            return ctx.enter_context(nc.sbuf_tensor(name, shape, dt))

        def sem(name):
            return ctx.enter_context(nc.semaphore(name))

        psum = ctx.enter_context(nc.psum_tensor("psum", [P, 8, 512], F32))

        identf = sb("identf", [P, P])
        ident = sb("ident", [P, P], BF16)
        tri = sb("tri", [P, P], BF16)
        ones = sb("ones", [P, P])
        halfneg = sb("halfneg", [P, GRP])
        idx_sb = sb("idx_sb", [P, TXT_TILES], I32)
        txt = sb("txt", [P, TXT_TILES, D])
        convw = sb("convw", [P, KT, D])
        posb = sb("posb", [P, NT, D])
        convb = sb("convb", [P, D])
        wat = sb("wat", [DH, 6, D + 1])
        pqkv = sb("pqkv", [DH, 6, DC])
        wqkv = sb("wqkv", [DH + 1, 2, 3, DC])
        wbt = sb("wbt", [DH, 2, CR])
        wpj = sb("wpj", [DH, 2, D])
        wout = sb("wout", [CR + 1, D])
        w1f = sb("w1f", [DH, 2, DFF])
        w2f = sb("w2f", [P, FT, D])
        w1q = sb("w1q", [DH, 2, DFF], BF16)
        w2q = sb("w2q", [P, FT, D], BF16)
        g1b = sb("g1b", [P, D])
        g2b = sb("g2b", [P, DFF])
        wsum = sb("wsum", [P, 2])
        wscale = sb("wscale", [P, 2])
        winv = sb("winv", [P, 2])
        wdq = sb("wdq", [P, 2])

        shared = sb("shared", [P, SHARED])
        taken = [0]

        def region(shape, dt=F32):
            size = int(np.prod(shape)) * (1 if dt == F32 else 2) // (1 if dt == F32 else 4)
            at = taken[0]
            taken[0] += size
            assert taken[0] <= SHARED
            flat = shared[:, at:at + size]
            if dt != F32:
                flat = flat.bitcast(dt)
            if len(shape) == 1:
                return flat
            names = "abcd"[:len(shape)]
            return flat.rearrange(f"p ({' '.join(names)}) -> p {' '.join(names)}",
                                  **{name: size for name, size in zip(names[:-1], shape)})

        xt = region([RING2, KT, W])
        hA = sb("hA", [P, RING2, GRP, D])
        bnA = sb("bnA", [P, GRP, 6])
        mvA = sb("mvA", [P, GRP, 2])
        veA = sb("veA", [P, GRP])
        rsA = sb("rsA", [P, GRP])
        zA = sb("zA", [P, GRP, D])
        zT = sb("zT", [DH + 1, 2, W])
        split = sb("split", [DC, 2, 3, W], BF16)
        rest = sb("rest", [DC, 2, W])
        vA = sb("vA", [P, H, GRP, VW, VP], BF16)
        vrest = sb("vrest", [P, GRP, H, HD])

        qs = sb("qs", [P, RING3, S], BF16)
        ks = sb("ks", [P, RING3, S], BF16)
        vs = sb("vs", [P, RING3, NTT, VW * VP], BF16)
        w32 = region([RING5, 512])
        whi = region([PCOLS], F16)
        wlo = region([PCOLS], F16)
        nmax = sb("nmax", [P, NTT + 1])
        nmrest = sb("nmrest", [P, NTT])
        nmparts = sb("nmparts", [P, NTT, 3], BF16)
        av = sb("av", [96, RING3, 512])
        cx = region([RING2, VP, S])[0:CR]
        cxs = sb("cxs", [CR, S])
        sums = sb("sums", [HEADS, S])
        rsums = sb("rsums", [HEADS, S])
        spread = sb("spread", [HEADS, RING2, CR])
        cxn = sb("cxn", [CR + 1, S])
        hB = sb("hB", [P, RING2, NTT, D])

        taken[0] = 0
        hC = region([RING3, CGRP, D])
        gl = region([CGRP, DFF])
        uF = region([RING3, CGRP, DFF])
        oC = region([RING3, CGRP, D])
        uC = region([CGRP, D])
        tC = region([CGRP, D])
        sq = region([DFF])
        xqF = region([CGRP, DFF], BF16)
        x2T = region([CGRP, FT, P], BF16)
        xqC = region([CGRP, D], BF16)
        x1T = region([2, CGRP * P], BF16)[0:DH]
        bnC = sb("bnC", [P, CGRP, 6])
        mvC = sb("mvC", [P, CGRP, 2])
        nC = sb("nC", [P, NORM, CGRP])
        peak1, peak2 = sb("peak1", [P, CGRP]), sb("peak2", [P, CGRP])
        qC = sb("qC", [P, 2, QUANT, CGRP])
        sumsq, meansq = sb("sumsq", [P, CGRP]), sb("meansq", [P, CGRP])
        rms2 = sb("rms2", [P, RING3, CGRP])

        idx_loaded, gathered = sem("idx_loaded"), sem("gathered")
        fold_loaded, embed_loaded, late_loaded = sem("fold_loaded"), sem("embed_loaded"), sem("late_loaded")
        const_step = sem("const_step")
        weights_step = sem("weights_step")
        folded, wsum_done = sem("folded"), sem("wsum_done")
        x_loaded = [sem("x_loaded0"), sem("x_loaded1")]
        conv_done, h_ready = sem("conv_done"), sem("h_ready")
        stats_done, aggr_done = sem("stats_done"), sem("aggr_done")
        eps_added, rstd_ready = sem("eps_added"), sem("rstd_ready")
        z_ready, zT_done, zT_copied = sem("z_ready"), sem("zT_done"), sem("zT_copied")
        qk_done, v_done = sem("qk_done"), sem("v_done")
        hi_ready, rest_ready = sem("hi_ready"), sem("rest_ready")
        mid_ready, lo_ready = sem("mid_ready"), sem("lo_ready")
        vhi_ready, vrest_ready, vmid_ready, v_copied = (sem("vhi_ready"), sem("vrest_ready"), sem("vmid_ready"),
                                                        sem("v_copied"))
        h_stored = [sem("h_stored0"), sem("h_stored1")]
        qk_stored, v_stored = sem("qk_stored"), sem("v_stored")
        qkv_loaded = [sem(f"qkv_loaded{i}") for i in range(RING3)]
        s1_done, s1_read = sem("s1_done"), sem("s1_read")
        parts_step, parts_ready = sem("parts_step"), sem("parts_ready")
        s2_done, exp_done = sem("s2_done"), sem("exp_done")
        maxT_done, maxT_in = sem("maxT_done"), sem("maxT_in")
        av_read = sem("av_read")
        lo_by_dve, lo_by_pool, av_step = sem("lo_by_dve"), sem("lo_by_pool"), sem("av_step")
        av_stored = [sem(f"av_stored{i}") for i in range(RING3)]
        batch_loaded = [sem("batch_loaded0"), sem("batch_loaded1")]
        cxs_step = sem("cxs_step")
        sums_loaded, rsums_ready = sem("sums_loaded"), sem("rsums_ready")
        spread_done, cxn_ready = sem("spread_done"), sem("cxn_ready")
        proj_done, h2_ready = sem("proj_done"), sem("h2_ready")
        h2_stored = [sem(f"h2_stored{i}") for i in range(RING2)]
        hC_loaded = [sem(f"hC_loaded{i}") for i in range(RING3)]
        statsC_done, aggrC_done, centred, peak1_done = (sem("statsC_done"), sem("aggrC_done"), sem("centred"),
                                                        sem("peak1_done"))
        norm_step = sem("norm_step")
        quant_step = [sem("quant_step0"), sem("quant_step1")]
        shifted1, ints1, shifted2, ints2 = sem("shifted1"), sem("ints1"), sem("shifted2"), sem("ints2")
        x1T_done, x1T_copied, up_done, gelu_done = sem("x1T_done"), sem("x1T_copied"), sem("up_done"), sem("gelu_done")
        squared, scaled, rms2_step, peak2_done = sem("squared"), sem("scaled"), sem("rms2_step"), sem("peak2_done")
        x2T_done, x2T_copied, down_done, out_done = sem("x2T_done"), sem("x2T_copied"), sem("down_done"), sem("out_done")
        out_stored = [sem(f"out_stored{i}") for i in range(RING3)]
        waits_met = sem("waits_met")

        block = ctx.enter_context(nc.Block())

        def own_wait(eng):
            eng.sem_inc(waits_met, 1)

        def stage_c(eng, step):
            step(0, 0, 0)
            with eng.Fori(0, CG // RING3 - 1) as i:
                for m in range(RING3):
                    step(i * RING3 + m + 1, (m + 1) % RING3, i + (m + 1) // RING3)
            for g in range(CG - RING3, CG):
                step(g, g % RING3, g // RING3)

        def ahead(by, g, r, lap):
            return g + by, (r + by) % RING3, lap + (r + by) // RING3

        def left(g):
            return min(CG - 1 - g, 2) if isinstance(g, int) else 2

        def stage_b(head_step, eng):
            for k in range(RING3):
                head_step(k, k, 0, k == 0, False)
            with eng.Fori(1, HEADS // RING3 - 1) as i:
                for k in range(RING3):
                    head_step(i * RING3 + k, k, i, False, False)
            for k in range(RING3):
                head_step(HEADS - RING3 + k, k, HEADS // RING3 - 1, False, k == RING3 - 1)

        def v_part(part, tiles):
            return vA[:, :, 0:tiles, 0:HD, part].rearrange("p h t c -> p t h c")

        def v_psum(tiles):
            return vP[:, 0:tiles, :].rearrange("p t (h c) -> p t h c", h=H)

        def low_part(eng, n, j, a, w):
            rows = P if j < NT else NTXT
            cols = slice(POFF[j] + a, POFF[j] + a + w)
            return eng.tensor_tensor(wlo[0:rows, cols], w32[0:rows, n % RING5, 0:w], whi[0:rows, cols], ALU.subtract)

        convP = [psum[:, i, 0:D] for i in range(RING2)]
        zTP = [psum[0:DH, 2 + a, :] for a in range(2)]
        qkP = [psum[0:DC, 4 + i, :] for i in range(2)]
        vP = psum[:, 6, 0:GRP * DC].rearrange("p (t c) -> p t c", t=GRP)
        s1P = [psum[:, 2 * i:2 * i + 2, :].rearrange("p a b -> p (a b)") for i in range(RING2)]
        s2P = [psum[:, 4 + i, :] for i in range(RING3)]
        avP = psum[0:96, 7, :]
        spreadP = [psum[0:CR, 4 + i, 0:S // 3] for i in range(RING3)]
        projP = [psum[:, i, 0:D] for i in range(RING3)]
        x1TP = psum[0:DH, 0, 0:CGRP * P].bitcast(BF16).rearrange("p (a t) -> p a t", a=2)
        upP = [psum[:, 1 + 2 * i:3 + 2 * i, 0:UPW] for i in range(RING2)]
        x2TP = [psum[:, 5 + i, 0:FT * P // 2].bitcast(BF16).rearrange("p (f t) -> p f t", f=FT) for i in range(RING2)]
        downP = [psum[:, 7, 0:D], psum[:, 7, D:2 * D], psum[:, 1, 0:D]]
        foldP = [psum[0:DH + 1, 4 + a, 0:3 * DC].rearrange("p (m c) -> p m c", m=3) for a in range(2)]
        woutP = psum[0:CR, 6, 0:D]
        wsumP = psum[:, 6, 0:2]

        @block.sync
        def _(sp):
            sp.dma_start(idx_sb[:], idx).then_inc(idx_loaded, 16)
            sp.dma_start(wat[:], w_attn).then_inc(fold_loaded, 16)
            sp.dma_start(pqkv[:, 0:2, :], p_q).then_inc(fold_loaded, 16)
            sp.dma_start(pqkv[:, 2:4, :], p_k).then_inc(fold_loaded, 16)
            sp.dma_start(pqkv[:, 4:6, :], p_v).then_inc(fold_loaded, 16)
            sp.dma_start(wbt[:], w_back).then_inc(fold_loaded, 16)
            sp.dma_start(wpj[:], w_proj).then_inc(fold_loaded, 16)
            sp.dma_start(convw[:], conv_w).then_inc(embed_loaded, 16)
            sp.dma_start(xt[:, 0], xT[0]).then_inc(x_loaded[0], 16)
            sp.dma_start(posb[:], pos).then_inc(embed_loaded, 16)
            sp.dma_start(convb[:], conv_b.partition_broadcast(P)).then_inc(embed_loaded, 16)
            sp.dma_start(g1b[:], g1.partition_broadcast(P)).then_inc(late_loaded, 16)
            sp.dma_start(g2b[:], g2.partition_broadcast(P)).then_inc(late_loaded, 16)
            sp.dma_start(wout[CR:CR + 1, :], b_proj).then_inc(late_loaded, 16)
            sp.dma_start(cxn[CR:CR + 1, :], row_of_ones).then_inc(late_loaded, 16)
            sp.dma_start(w1f[:], w1).then_inc(late_loaded, 16)
            sp.dma_start(w2f[:], w2).then_inc(late_loaded, 16)
            sp.dma_start(xt[:, 1], xT[1]).then_inc(x_loaded[1], 16)

            def store_group(g, b, half, tiles):
                lo, hi = half * W, half * W + W
                if b is None:
                    sp.wait_ge(h_ready, RING2 + NGRP * GRP + tiles)
                    for t in range(tiles):
                        for bb in range(GRP):
                            sp.dma_start(h_dram[GRP * t + bb, NPATCH:S, :],
                                         hA[NTXT * bb:NTXT * bb + NTXT, 0, t, :]).then_inc(h_stored[0], 16)
                else:
                    sp.wait_ge(h_ready, g * GRP + RING2 + tiles)
                    sp.dma_start(h_dram[bass.ds(b, 1), lo:hi, :].rearrange("a (t p) d -> (a p) t d", p=P),
                                 hA[:, half]).then_inc(h_stored[half], 16)
                sp.wait_ge(hi_ready, g * 2 + 2)
                sp.wait_ge(mid_ready, g * 2 + 2)
                sp.wait_ge(lo_ready, g * 2 + 2)
                for which, dram, parts in ((0, q_dram, PARTS_Q), (1, k_dram, PARTS_K)):
                    for slot in range(NPART):
                        src = split[:, which, parts[slot], :]
                        if b is None:
                            sp.dma_start(dram[:, slot, NPATCH:S].rearrange("(b p) t -> p b t", b=B),
                                         src[:, 0:B * NTXT].rearrange("p (b t) -> p b t", b=B)).then_inc(qk_stored, 16)
                        else:
                            sp.dma_start(dram[bass.ds(b * DC, DC), slot, lo:hi], src).then_inc(qk_stored, 16)
                sp.wait_ge(v_copied, g + 2)
                if b is None:
                    for t in range(tiles):
                        for bb in range(GRP):
                            sp.dma_start(v_dram[GRP * t + bb, :, 0:NTXT, NT].rearrange("h p c v -> p h (c v)"),
                                         vA[NTXT * bb:NTXT * bb + NTXT, :, t].rearrange("p h c v -> p h (c v)")).then_inc(v_stored, 16)
                else:
                    sp.dma_start(v_dram[bass.ds(b, 1), :, :, half * GRP:half * GRP + GRP]
                                 .rearrange("a h p t c v -> (a p) h (t c v)"),
                                 vA[:].rearrange("p h t c v -> p h (t c v)")).then_inc(v_stored, 16)

            def batch_stores(b, prefetch):
                for half in range(HALVES):
                    g = b * HALVES + half
                    if prefetch:
                        sp.wait_ge(conv_done, g * GRP + GRP)
                        sp.dma_start(xt[:, half], xT[bass.ds(g + RING2, 1)].rearrange("a p k t -> (a p) k t")
                                     ).then_inc(x_loaded[half], 16)
                    store_group(g, b, half, GRP)

            with sp.Fori(0, B - 1) as b:
                batch_stores(b, True)
            batch_stores(B - 1, False)
            store_group(NGRP, None, 0, TXT_TILES)

            sp.wait_ge(h_stored[0], 16 * (1 + B + B))
            sp.wait_ge(h_stored[1], 16 * (1 + B))
            sp.wait_ge(qk_stored, 16 * 2 * NPART * (1 + NGRP + 1))
            sp.wait_ge(v_stored, 16 * (1 + NGRP + B))
            sp.wait_ge(const_step, FILLED)

            def load_head(seq, k):
                for ring, dram in ((qs, q_dram), (ks, k_dram)):
                    sp.dma_start(ring[0:KROWS, k, :], dram[bass.ds(seq * HD, HD)].rearrange("r s t -> (r s) t")
                                 ).then_inc(qkv_loaded[k], 16)
                v_head = v_dram.rearrange("b h p t c v -> (b h) p t (c v)")[bass.ds(seq, 1)]
                sp.dma_start(vs[:, k, 0:NT, :], v_head[:, :, 0:NT].rearrange("a p t c -> (a p) t c")
                             ).then_inc(qkv_loaded[k], 16)
                sp.dma_start(vs[0:NTXT, k, NT, :], v_head[:, 0:NTXT, NT].rearrange("a p c -> (a p) c")
                             ).then_inc(qkv_loaded[k], 16)

            for k in range(RING3):
                load_head(k, k)

            def head_io(seq, k, lap, first, last):
                sp.wait_ge(av_read, seq + 2)
                for r, (q0, w) in enumerate(RUNS):
                    sp.dma_start(c_dram[bass.ds(seq, 1), :, q0:q0 + w].rearrange("a r t -> (a r) t"),
                                 av[32 * r:32 * r + VW * VP, k, 0:w]).then_inc(av_stored[k], 16)
                if not isinstance(seq, int) or seq < HEADS - RING3:
                    load_head(seq + RING3, k)

            stage_b(head_io, sp)

            for k in range(RING3):
                sp.wait_ge(av_stored[k], 48 * (1 + HEADS // RING3))

            sp.dma_start(sums[:], c_dram[:, HD * VP, :]).then_inc(sums_loaded, 16)

            def load_batch(b, k):
                sp.dma_start(spread[:, k, :], spread_rows[bass.ds(b, 1)].rearrange("a r c -> (a r) c")
                             ).then_inc(batch_loaded[k], 16)
                sp.dma_start(cx[:, k], c_dram[bass.ds(b * H, H)].rearrange("h (r v) t -> (h r) v t", v=VP)
                             ).then_inc(batch_loaded[k], 16)
                sp.dma_start(hB[:, k, 0:NT, :],
                             h_dram[bass.ds(b, 1), 0:NPATCH, :].rearrange("a (t p) d -> (a p) t d", p=P)
                             ).then_inc(batch_loaded[k], 16)
                sp.dma_start(hB[0:NTXT, k, NT, :], h_dram[bass.ds(b, 1), NPATCH:S, :].rearrange("a t d -> (a t) d")
                             ).then_inc(batch_loaded[k], 16)

            def store_batch(b, k, lap, more):
                sp.wait_ge(h2_ready, b * NTT + NTT + RING3)
                rows = b * S
                image = slice(rows, rows + NPATCH) if isinstance(b, int) else bass.ds(rows, NPATCH)
                text = slice(rows + NPATCH, rows + S) if isinstance(b, int) else bass.ds(rows + NPATCH, NTXT)
                sp.dma_start(h2_dram[image, :].rearrange("(t p) d -> p t d", p=P), hB[:, k, 0:NT, :]
                             ).then_inc(h2_stored[k], 16)
                sp.dma_start(h2_dram[text, :], hB[0:NTXT, k, NT, :]).then_inc(h2_stored[k], 16)
                if more:
                    sp.wait_ge(h2_stored[k], lap * 32 + 32)
                    load_batch(b + RING2, k)

            for k in range(RING2):
                load_batch(k, k)
            with sp.Fori(0, B // RING2 - 1) as i:
                for k in range(RING2):
                    store_batch(i * RING2 + k, k, i, True)
            for k in range(RING2):
                sp.wait_ge(h2_stored[k], 32 * (B // RING2 - 1))
            def load_group(rows, r):
                sp.dma_start(hC[:, r], h2_dram[rows, :].rearrange("(k p) d -> p k d", p=P)).then_inc(hC_loaded[r], 16)

            for g in range(RING3):
                load_group(slice(g * CGRP * P, (g + 1) * CGRP * P), g)
            for k in range(RING2):
                store_batch(B - RING2 + k, k, B // RING2 - 1, False)

            for k in range(RING2):
                sp.wait_ge(h2_stored[k], 32 * (B // RING2))

            def group_io(g, r, lap):
                sp.wait_ge(out_done, g * CGRP + 2 * CGRP)
                rows = slice(g * CGRP * P, (g + 1) * CGRP * P) if isinstance(g, int) else bass.ds(g * (CGRP * P), CGRP * P)
                sp.dma_start(out[rows, :].rearrange("(k p) d -> p k d", p=P), oC[:, r]).then_inc(out_stored[r], 16)
                if not isinstance(g, int) or g < CG - RING3:
                    load_group(bass.ds((g + RING3) * (CGRP * P), CGRP * P), r)

            stage_c(sp, group_io)
            for r in range(RING3):
                sp.wait_ge(out_stored[r], 16 * (1 + len(range(r, CG, RING3))))

        @block.gpsimd
        def _(pool):
            for s, n in ((h_ready, RING2), (h_stored[0], 16), (h_stored[1], 16), (zT_done, 1), (zT_copied, 2), (v_done, 1),
                         (rest_ready, 2), (v_copied, 1), (qk_stored, 16 * 2 * NPART), (v_stored, 16),
                         (s1_read, RING2), (maxT_in, 2), (exp_done, RING3), (av_read, 1), *((q, 48) for q in av_stored), (av_step, NTT),
                         (lo_by_dve, RING5), (lo_by_pool, RING5), (cxn_ready, 3), (proj_done, NTT), (h2_ready, RING3),
                         *((q, 16) for q in out_stored), (x1T_done, 1), (x1T_copied, 1), (gelu_done, CGRP), (squared, 1),
                         (scaled, CGRP), (rms2_step, 2), (ints2, RING3 * CGRP), (x2T_done, CGRP), (x2T_copied, CGRP),
                         (out_done, CGRP)):
                pool.sem_inc(s, n)
            nc.gpsimd.memset(ident[:], 0.0).then_inc(const_step, 1)
            nc.gpsimd.memset(identf[:], 0.0).then_inc(const_step, 1)
            nc.gpsimd.memset(tri[:], 0.0).then_inc(const_step, 1)
            nc.gpsimd.memset(halfneg[:], -0.5).then_inc(const_step, 1)
            pool.wait_ge(const_step, 4)
            nc.gpsimd.affine_select(out=ident[:], in_=ident[:], compare_op=ALU.not_equal, fill=1.0, base=0,
                                    pattern=[[-1, P]], channel_multiplier=1).then_inc(const_step, 1)
            nc.gpsimd.affine_select(out=identf[:], in_=identf[:], compare_op=ALU.not_equal, fill=1.0, base=0,
                                    pattern=[[-1, P]], channel_multiplier=1).then_inc(const_step, 1)
            nc.gpsimd.affine_select(out=tri[:], in_=tri[:], compare_op=ALU.is_ge, fill=NEG, base=0,
                                    pattern=[[1, P]], channel_multiplier=-1).then_inc(const_step, 1)
            pool.wait_ge(idx_loaded, 16)
            for t in range(TXT_TILES):
                nc.gpsimd.indirect_dma_start(out=txt[:, t, :], out_offset=None, in_=emb,
                                             in_offset=bass.IndirectOffsetOnAxis(ap=idx_sb[:, t:t + 1], axis=0)
                                             ).then_inc(gathered, 16)

            for n, (ap, value) in enumerate(((qs[32:64], 0.0), (qs[64:MROW], 0.0), (qs[MROW:P], EXP_SHIFT),
                                             (ks[32:64], 0.0), (ks[64:MROW], 0.0), (ks[MROW:P], 1.0))):
                pool.wait_ge(const_step, CONSTANTS + n)
                nc.gpsimd.memset(ap, value).then_inc(const_step, 1)
            pool.wait_ge(const_step, FILLED)

            def rstd_group(g, tiles):
                pool.wait_ge(aggr_done, g + 1)
                own_wait(pool)
                nc.gpsimd.tensor_scalar(veA[:, 0:tiles], mvA[:, 0:tiles, 1], LN_EPS, None, ALU.add
                                        ).then_inc(eps_added, 1)
                pool.wait_ge(eps_added, g + 1)
                nc.gpsimd.tensor_tensor(rsA[:, 0:tiles], veA[:, 0:tiles], halfneg[:, 0:tiles], ALU.pow
                                        ).then_inc(rstd_ready, 1)

            with pool.Fori(0, NGRP) as g:
                rstd_group(g, GRP)
            rstd_group(NGRP, TXT_TILES)

            def low_parts(seq, k, lap, first, last):
                for m, n in enumerate(POOL_CHUNKS):
                    j, a, w = CHUNKS[n]
                    pool.wait_ge(exp_done, seq * NS2 + n + 1 + RING3)
                    low_part(nc.gpsimd, n, j, a, w).then_inc(lo_by_pool, 1)

            stage_b(low_parts, pool)

            def sum_parts(b, k, lap):
                pool.wait_ge(batch_loaded[k], lap * 64 + 64)
                pool.wait_ge(cxn_ready, b * 3 + 3)
                nc.gpsimd.tensor_tensor(cxs[:], cx[:, k, 0, :], cx[:, k, 1, :], ALU.add).then_inc(cxs_step, 1)
                pool.wait_ge(cxs_step, b * 2 + 1)
                nc.gpsimd.tensor_tensor(cxs[:], cxs[:], cx[:, k, 2, :], ALU.add).then_inc(cxs_step, 1)

            with pool.Fori(0, B // RING2) as i:
                for k in range(RING2):
                    sum_parts(i * RING2 + k, k, i)

            def norm_group(g):
                def link(m, ins):
                    ins.then_inc(norm_step, 1)
                    pool.wait_ge(norm_step, g * NORM + m + 1)

                var = mvC[:, :, 1]
                pool.wait_ge(aggrC_done, g + 1)
                own_wait(pool)
                link(0, nc.gpsimd.tensor_scalar(nC[:, 0], var, LN_EPS, None, ALU.add))
                link(1, nc.gpsimd.tensor_tensor(nC[:, 1], nC[:, 0], halfneg[:, 0:CGRP], ALU.pow))
                link(2, nc.gpsimd.tensor_tensor(nC[:, 2], var, nC[:, 1], ALU.mult))
                link(3, nc.gpsimd.tensor_tensor(nC[:, 3], nC[:, 2], nC[:, 1], ALU.mult))
                own_wait(pool)
                link(4, nc.gpsimd.tensor_scalar(nC[:, 4], nC[:, 3], RMS_EPS, None, ALU.add))
                link(5, nc.gpsimd.tensor_tensor(nC[:, 5], nC[:, 4], halfneg[:, 0:CGRP], ALU.pow))
                nc.gpsimd.tensor_tensor(nC[:, 6], nC[:, 5], nC[:, 1], ALU.mult).then_inc(norm_step, 1)

            def hidden_group(g, r, follows):
                for k in range(CGRP):
                    n = g * CGRP + k
                    pool.wait_ge(gelu_done, n + 1 + CGRP)
                    pool.wait_ge(ints2, n + 1)
                    nc.gpsimd.tensor_tensor(uF[:, r, k, :], gl[:, k, :], g2b[:], ALU.mult).then_inc(scaled, 1)
                if follows:
                    norm_group(g + 1)
                pool.wait_ge(squared, g * CGRP + CGRP + 1)
                own_wait(pool)
                nc.gpsimd.tensor_scalar(meansq[:], sumsq[:], 1.0 / DFF, RMS_EPS, ALU.mult, ALU.add).then_inc(rms2_step, 1)
                pool.wait_ge(rms2_step, g * 2 + 1 + 2)
                nc.gpsimd.tensor_tensor(rms2[:, r], meansq[:], halfneg[:, 0:CGRP], ALU.pow).then_inc(rms2_step, 1)

            def norms(g, r, lap):
                if left(g):
                    g1, r1, lap1 = ahead(1, g, r, lap)
                    hidden_group(g1, r1, left(g) > 1)

            norm_group(0)
            hidden_group(0, 0, True)
            stage_c(pool, norms)

        @block.scalar
        def _(act):
            def group_a(g, tiles):
                cols = tiles * P
                act.wait_ge(zT_done, g + 2)
                act.wait_ge(v_done, g + 1)
                for a in range(2):
                    nc.scalar.copy(zT[0:DH, a, 0:cols], zTP[a][:, 0:cols]).then_inc(zT_copied, 1)
                act.wait_ge(qk_stored, g * (16 * 2 * NPART) + 16 * 2 * NPART)
                for which in range(2):
                    act.wait_ge(qk_done, g * 2 + which + 1)
                    nc.scalar.copy(split[:, which, 0, 0:cols], qkP[which][:, 0:cols]).then_inc(hi_ready, 1)
                act.wait_ge(v_done, g + 2)
                act.wait_ge(v_stored, g * 16 + 16)
                nc.scalar.copy(v_part(0, tiles), v_psum(tiles)).then_inc(vhi_ready, 1)

            act.wait_ge(weights_step, FOLD_STEPS)
            group_a(0, GRP)
            with act.Fori(1, NGRP) as g:
                group_a(g, GRP)
            group_a(NGRP, TXT_TILES)

            def maxima_in(seq, k):
                act.wait_ge(maxT_done, seq * 2 + 1)
                nc.scalar.copy(qs[MROW:MROW + 3, k, 0:NPATCH], s1P[0][MROW:MROW + 3, :]).then_inc(maxT_in, 1)
                act.wait_ge(maxT_done, seq * 2 + 2)
                nc.scalar.copy(qs[MROW:MROW + 3, k, NPATCH:S], s1P[1][MROW:MROW + 3, 0:NTXT]).then_inc(maxT_in, 1)

            def av_out(seq, k, lap):
                act.wait_ge(av_step, seq * NTT + NTT + NTT)
                act.wait_ge(av_stored[k], lap * 48 + 48)
                nc.scalar.copy(av[:, k, :], avP).then_inc(av_read, 1)

            def exps(seq, k, lap, first, last):
                for n, (j, a, w) in enumerate(CHUNKS):
                    rows = P if j < NT else NTXT
                    cols = slice(POFF[j] + a, POFF[j] + a + w)
                    act.wait_ge(s2_done, seq * NS2 + n + 1)
                    d, p = low_counts(n - RING5)
                    act.wait_ge(lo_by_dve, seq * len(DVE_CHUNKS) + d + RING5)
                    act.wait_ge(lo_by_pool, seq * len(POOL_CHUNKS) + p + RING5)
                    nc.scalar.activation(w32[0:rows, n % RING5, 0:w], s2P[n % RING3][0:rows, 0:w], ACT.Exp)
                    if a == 0:
                        act.wait_ge(av_step, seq * NTT + NT - j + 1)
                    nc.scalar.activation(whi[0:rows, cols], s2P[n % RING3][0:rows, 0:w], ACT.Exp).then_inc(exp_done, 1)
                    if n == AV_OUT_AT and not first:
                        av_out(seq - 1, (k - 1) % RING3, lap if k else lap - 1)
                    if n == MAXIMA_IN_AT and not last:
                        maxima_in(seq + 1, (k + 1) % RING3)
                if last:
                    av_out(seq, k, lap)

            act.wait_ge(weights_step, WEIGHT_STEPS)
            maxima_in(0, 0)
            stage_b(exps, act)

            def hidden_group(g):
                act.wait_ge(x1T_done, g + 2)
                nc.scalar.copy(x1T, x1TP).then_inc(x1T_copied, 1)
                act.wait_ge(quant_step[0], g * QUANT + QUANT)
                for k in range(CGRP):
                    n = g * CGRP + k
                    act.wait_ge(up_done, n + 1)
                    act.wait_ge(scaled, n + 1)
                    nc.scalar.activation(gl[:, k, :].rearrange("p (a f) -> p a f", a=2), upP[TWO_PLACES[k]], ACT.Gelu,
                                         scale=qC[:, 0, 4, k:k + 1]).then_inc(gelu_done, 1)

            def square(g, k):
                n = g * CGRP + k
                act.wait_ge(gelu_done, n + 1 + CGRP)
                act.wait_ge(squared, n + 1)
                if k == 0:
                    act.wait_ge(rms2_step, g * 2 + 2)
                nc.scalar.activation(sq, gl[:, k, :], ACT.Square, accum_out=sumsq[:, k:k + 1]).then_inc(squared, 1)

            def hidden_and_down(g, r, lap):
                if left(g):
                    hidden_group(g + 1)
                for k in range(CGRP):
                    act.wait_ge(x2T_done, g * CGRP + k + 1 + CGRP)
                    nc.scalar.copy(x2T[:, k], x2TP[TWO_PLACES[k]]).then_inc(x2T_copied, 1)
                    if left(g):
                        square(g + 1, k)

            hidden_group(0)
            for k in range(CGRP):
                square(0, k)
            stage_c(act, hidden_and_down)

        @block.vector
        def _(dve):
            count = [0]

            def link(ins):
                count[0] += 1
                ins.then_inc(weights_step, 1)
                dve.wait_ge(weights_step, count[0])

            for ap, value in ((ones[:], 1.0), (zT[DH:DH + 1, 1, :], 1.0), (vA[:, :, :, HD, 0], 1.0),
                              (vA[:, :, :, HD, 1], 0.0), (vA[:, :, :, HD, 2], 0.0), (psum[:, 7, :], 0.0),
                              (nmax[:], 0.0)):
                link(nc.vector.memset(ap, value))
            dve.wait_ge(embed_loaded, 16 * EMBED_LOADS)
            for t in range(NT):
                link(nc.vector.tensor_tensor(posb[:, t, :], posb[:, t, :], convb[:], ALU.add))
            dve.wait_ge(folded, 1)
            for m in range(3):
                factor = HD ** -0.5 if m == 0 else 1.0
                for a in range(2):
                    link(nc.vector.tensor_scalar(wqkv[0:DH + a, a, m, :], foldP[a][0:DH + a, m, :], factor, None, ALU.mult))
            link(nc.vector.tensor_copy(wout[0:CR, :], woutP))
            assert count[0] == FOLD_STEPS

            def embed_group(b, half, tiles, text):
                n0 = (b * HALVES + half) * GRP
                for t in range(tiles):
                    if text:
                        if t == 0:
                            dve.wait_ge(gathered, 16 * TXT_TILES)
                            dve.wait_ge(h_stored[0], 16 * B + 16)
                        nc.vector.tensor_copy(hA[:, half, t, :], txt[:, t, :]).then_inc(h_ready, 1)
                    else:
                        if t == 0:
                            dve.wait_ge(h_stored[half], b * 16 + 16)
                        dve.wait_ge(conv_done, n0 + t + 1)
                        nc.vector.tensor_tensor(hA[:, half, t, :], convP[t % RING2], posb[:, half * GRP + t, :], ALU.add
                                                ).then_inc(h_ready, 1)
                for t in range(tiles):
                    dve.wait_ge(h_ready, n0 + t + 1 + RING2)
                    nc.vector.bn_stats(bnA[:, t, :], hA[:, half, t, :]).then_inc(stats_done, 1)
                for t in range(tiles):
                    dve.wait_ge(stats_done, n0 + t + 1)
                    own_wait(dve)
                    last = nc.vector.bn_aggr(mvA[:, t, :], bnA[:, t, :])
                last.then_inc(aggr_done, 1)

            def normalise_group(g, half, tiles):
                dve.wait_ge(rstd_ready, g + 1)
                dve.wait_ge(zT_done, g + 1)
                for t in range(tiles):
                    nc.vector.tensor_scalar(zA[:, t, :], hA[:, half, t, :], mvA[:, t, 0:1], rsA[:, t:t + 1],
                                            ALU.subtract, ALU.mult).then_inc(z_ready, 1)

            def split_group(g, tiles):
                cols = tiles * P
                for which in range(2):
                    hi, mid, lo = (split[:, which, part, 0:cols] for part in range(3))
                    n = g * 2 + which + 1
                    dve.wait_ge(hi_ready, n)
                    nc.vector.tensor_tensor(rest[:, which, 0:cols], qkP[which][:, 0:cols], hi, ALU.subtract
                                            ).then_inc(rest_ready, 1)
                    dve.wait_ge(rest_ready, n + 2)
                    nc.vector.tensor_copy(mid, rest[:, which, 0:cols]).then_inc(mid_ready, 1)
                    dve.wait_ge(mid_ready, n)
                    nc.vector.tensor_tensor(lo, rest[:, which, 0:cols], mid, ALU.subtract).then_inc(lo_ready, 1)
                dve.wait_ge(vhi_ready, g + 1)
                nc.vector.tensor_tensor(vrest[:, 0:tiles], v_psum(tiles), v_part(0, tiles), ALU.subtract
                                        ).then_inc(vrest_ready, 1)
                dve.wait_ge(vrest_ready, g + 1)
                nc.vector.tensor_copy(v_part(1, tiles), vrest[:, 0:tiles]).then_inc(vmid_ready, 1)
                dve.wait_ge(vmid_ready, g + 1)
                nc.vector.tensor_tensor(v_part(2, tiles), vrest[:, 0:tiles], v_part(1, tiles), ALU.subtract
                                        ).then_inc(v_copied, 1)

            embed_group(0, 0, GRP, False)
            with dve.Fori(0, B - 1) as b:
                for half in range(HALVES):
                    g = b * HALVES + half
                    normalise_group(g, half, GRP)
                    embed_group(b + half, 1 - half, GRP, False)
                    split_group(g, GRP)
            for g in range(NGRP - HALVES, NGRP):
                half = g % HALVES
                normalise_group(g, half, GRP)
                if g < NGRP - 1:
                    embed_group(B - 1, 1 - half, GRP, False)
                else:
                    embed_group(B, 0, TXT_TILES, True)
                split_group(g, GRP)
            normalise_group(NGRP, 0, TXT_TILES)
            split_group(NGRP, TXT_TILES)

            dve.wait_ge(late_loaded, 16 * LATE_LOADS)
            link(nc.vector.tensor_reduce(wsum[0:DH, 0:1], w1f[:].rearrange("p a f -> p (a f)"), AX_X, ALU.add,
                                         apply_absolute_value=True))
            link(nc.vector.tensor_reduce(wsum[:, 1:2], w2f[:].rearrange("p a f -> p (a f)"), AX_X, ALU.add,
                                         apply_absolute_value=True))
            assert count[0] == SUM_STEPS
            dve.wait_ge(wsum_done, 1)
            link(nc.vector.tensor_scalar(wscale[:], wsumP, 1.0 / (D * DFF), Q_EPS, ALU.mult, ALU.max))
            link(nc.vector.reciprocal(winv[:], wscale[:]))
            link(nc.vector.tensor_scalar(wdq[:], wscale[:], 1.0 / 127.0, None, ALU.mult))
            for n, (wf, wq, rows) in enumerate(((w1f, w1q, DH), (w2f, w2q, P))):
                link(nc.vector.tensor_scalar(wf[:], wf[:], winv[0:rows, n:n + 1], 1.0, ALU.mult, ALU.min))
                link(nc.vector.tensor_scalar(wf[:], wf[:], -1.0, MAGIC, ALU.max, ALU.add))
                link(nc.vector.tensor_scalar(wq[:], wf[:], MAGIC, None, ALU.subtract))
            assert count[0] == WEIGHT_STEPS

            def maxima(seq, uses):
                for u in uses:
                    i, k0, w = S1_USES[u]
                    rows = P if i < NT else NTXT
                    col = i + (k0 > 0)
                    dve.wait_ge(s1_done, seq * NS1 + u + 1)
                    nc.vector.tensor_reduce(nmax[0:rows, col:col + 1], s1P[u % RING2][0:rows, 0:w], AX_X, ALU.max,
                                            negate=True).then_inc(s1_read, 1)

            def split_maxima(seq):
                dve.wait_ge(s1_read, seq * NS1 + NS1 + RING2)
                nc.vector.tensor_tensor(nmax[0:NTXT, NT:NTT], nmax[0:NTXT, NT:NTT], nmax[0:NTXT, NTT:NTT + 1], ALU.min
                                        ).then_inc(parts_step, 1)
                dve.wait_ge(parts_step, seq * 4 + 1)
                nc.vector.tensor_copy(nmparts[:, :, 0], nmax[:, 0:NTT]).then_inc(parts_step, 1)
                dve.wait_ge(parts_step, seq * 4 + 2)
                nc.vector.tensor_tensor(nmrest[:], nmax[:, 0:NTT], nmparts[:, :, 0], ALU.subtract).then_inc(parts_step, 1)
                dve.wait_ge(parts_step, seq * 4 + 3)
                nc.vector.tensor_copy(nmparts[:, :, 1], nmrest[:]).then_inc(parts_step, 1)
                dve.wait_ge(parts_step, seq * 4 + 4)
                nc.vector.tensor_tensor(nmparts[:, :, 2], nmrest[:], nmparts[:, :, 1], ALU.subtract
                                        ).then_inc(parts_ready, 1)

            def weights_and_maxima(seq, k, lap, first, last):
                for n in range(NS2 + 1):
                    uses = S1_AFTER.get(n, ())
                    if not last:
                        maxima(seq + 1, uses)
                        if NS1 - 1 in uses:
                            split_maxima(seq + 1)
                    if n - 1 in DVE_CHUNKS:
                        j, a, w = CHUNKS[n - 1]
                        dve.wait_ge(exp_done, seq * NS2 + n + RING3)
                        low_part(nc.vector, n - 1, j, a, w).then_inc(lo_by_dve, 1)

            maxima(0, range(NS1))
            split_maxima(0)
            stage_b(weights_and_maxima, dve)

            def normalise(b, k, lap):
                dve.wait_ge(cxs_step, b * 2 + 2)
                for c in range(3):
                    n = b * 3 + c
                    cols = slice(c * (S // 3), (c + 1) * (S // 3))
                    dve.wait_ge(spread_done, n + 1)
                    if c == 0:
                        dve.wait_ge(proj_done, b * NTT + NTT)
                    nc.vector.tensor_tensor(cxn[0:CR, cols], cxs[:, cols], spreadP[c], ALU.mult).then_inc(cxn_ready, 1)
                for t in range(NTT):
                    n = b * NTT + t
                    rows = P if t < NT else NTXT
                    dve.wait_ge(proj_done, n + 1 + NTT)
                    nc.vector.tensor_tensor(hB[0:rows, k, t, :], projP[t % RING3][0:rows], hB[0:rows, k, t, :], ALU.add
                                            ).then_inc(h2_ready, 1)

            dve.wait_ge(sums_loaded, 16)
            nc.vector.reciprocal(rsums[:], sums[:]).then_inc(rsums_ready, 1)
            with dve.Fori(0, B // RING2) as i:
                for k in range(RING2):
                    dve.wait_ge(batch_loaded[k], i * 64 + 64)
                    normalise(i * RING2 + k, k, i)

            def centre_group(g, r, lap):
                dve.wait_ge(hC_loaded[r], lap * 16 + 16)
                for k in range(CGRP):
                    nc.vector.bn_stats(bnC[:, k, :], hC[:, r, k, :]).then_inc(statsC_done, 1)
                for k in range(CGRP):
                    dve.wait_ge(statsC_done, g * CGRP + k + 1)
                    own_wait(dve)
                    last = nc.vector.bn_aggr(mvC[:, k, :], bnC[:, k, :])
                last.then_inc(aggrC_done, 1)
                dve.wait_ge(aggrC_done, g + 1)
                for k in range(CGRP):
                    nc.vector.scalar_tensor_tensor(out=uC[:, k, :], in0=hC[:, r, k, :], scalar=mvC[:, k, 0:1], in1=g1b[:],
                                                   op0=ALU.subtract, op1=ALU.mult).then_inc(centred, 1)
                for k in range(CGRP):
                    dve.wait_ge(centred, g * CGRP + k + 1)
                    nc.vector.tensor_reduce(peak1[:, k:k + 1], uC[:, k, :], AX_X, ALU.max, apply_absolute_value=True
                                            ).then_inc(peak1_done, 1)

            def scales(g, which, peak, factor):
                q = qC[:, which]

                def link(m, ins):
                    ins.then_inc(quant_step[which], 1)
                    dve.wait_ge(quant_step[which], g * QUANT + m + 1)

                link(0, nc.vector.tensor_tensor(q[:, 0], peak, factor, ALU.mult))
                link(1, nc.vector.tensor_scalar(q[:, 1], q[:, 0], Q_EPS, None, ALU.max))
                link(2, nc.vector.reciprocal(q[:, 2], q[:, 1]))
                link(3, nc.vector.scalar_tensor_tensor(out=q[:, 3], in0=q[:, 2], scalar=127.0, in1=factor,
                                                       op0=ALU.mult, op1=ALU.mult))
                nc.vector.tensor_scalar(q[:, 4], q[:, 1], wdq[:, which:which + 1], None, ALU.mult
                                        ).then_inc(quant_step[which], 1)

            def integers_of_tokens(g):
                dve.wait_ge(peak1_done, g * CGRP + CGRP)
                dve.wait_ge(norm_step, g * NORM + NORM)
                scales(g, 0, peak1[:], nC[:, 6])
                for k in range(CGRP):
                    nc.vector.tensor_scalar(tC[:, k, :], uC[:, k, :], qC[:, 0, 3, k:k + 1], MAGIC, ALU.mult, ALU.add
                                            ).then_inc(shifted1, 1)
                dve.wait_ge(x1T_done, g + 1)
                for k in range(CGRP):
                    dve.wait_ge(shifted1, g * CGRP + k + 1)
                    nc.vector.tensor_scalar(xqC[:, k, :], tC[:, k, :], MAGIC, None, ALU.subtract).then_inc(ints1, 1)

            def integers_of_hidden(g, r):
                dve.wait_ge(peak2_done, g * CGRP + CGRP)
                dve.wait_ge(rms2_step, g * 2 + 2 + 2)
                scales(g, 1, peak2[:], rms2[:, r])
                for k in range(CGRP):
                    nc.vector.tensor_scalar(uF[:, r, k, :], uF[:, r, k, :], qC[:, 1, 3, k:k + 1], MAGIC, ALU.mult, ALU.add
                                            ).then_inc(shifted2, 1)
                for k in range(CGRP):
                    dve.wait_ge(shifted2, g * CGRP + k + 1)
                    dve.wait_ge(x2T_done, g * CGRP + k + 1)
                    nc.vector.tensor_scalar(xqF[:, k, :], uF[:, r, k, :], MAGIC, None, ALU.subtract).then_inc(ints2, 1)

            def output_group(g, r, lap):
                dve.wait_ge(out_stored[r], lap * 16 + 16)
                dve.wait_ge(quant_step[1], g * QUANT + QUANT)
                for k in range(CGRP):
                    dve.wait_ge(down_done, g * CGRP + max(k + 1, 2))
                    nc.vector.scalar_tensor_tensor(out=oC[:, r, k, :], in0=downP[k], scalar=qC[:, 1, 4, k:k + 1],
                                                   in1=hC[:, r, k, :], op0=ALU.mult, op1=ALU.add).then_inc(out_done, 1)

            def peaks_of_hidden(g, r):
                for k in range(CGRP):
                    dve.wait_ge(scaled, g * CGRP + k + 1 + CGRP)
                    nc.vector.tensor_reduce(peak2[:, k:k + 1], uF[:, r, k, :], AX_X, ALU.max, apply_absolute_value=True
                                            ).then_inc(peak2_done, 1)

            def quantise(g, r, lap):
                if left(g):
                    integers_of_tokens(g + 1)
                integers_of_hidden(g, r)
                if left(g) > 1:
                    centre_group(*ahead(2, g, r, lap))
                if left(g):
                    peaks_of_hidden(g + 1, (r + 1) % RING3)
                output_group(g, r, lap)

            centre_group(0, 0, 0)
            integers_of_tokens(0)
            centre_group(1, 1, 0)
            peaks_of_hidden(0, 0)
            stage_c(dve, quantise)

        @block.tensor
        def _(pe):
            mm = nc.tensor.matmul
            pe.wait_ge(fold_loaded, 16 * FOLD_LOADS)
            for a in range(2):
                for m in range(3):
                    for jj in range(2):
                        mm(foldP[a][0:DH + a, m, :], wat[:, 2 * m + jj, a * DH:a * DH + DH + a], pqkv[:, 2 * m + jj, :],
                           start=jj == 0, stop=jj == 1)
            for jj in range(2):
                last = mm(woutP, wbt[:, jj, :], wpj[:, jj, :], start=jj == 0, stop=jj == 1)
            last.then_inc(folded, 1)
            pe.wait_ge(embed_loaded, 16 * EMBED_LOADS)

            def convolve_tiles(g, half, lap, tiles):
                n0 = g * GRP
                pe.wait_ge(x_loaded[half], lap * 16 + 16)
                for t in tiles:
                    pe.wait_ge(h_ready, n0 + t + 1)
                    for k in range(KT):
                        last = mm(convP[t % RING2], xt[:, half, k, t * P:t * P + P], convw[:, k, :],
                                  start=k == 0, stop=k == KT - 1)
                    last.then_inc(conv_done, 1)

            def qkv_group(g, tiles, following=None):
                n0 = g * GRP
                pe.wait_ge(zT_copied, g * 2 + 2)
                for t in range(tiles):
                    pe.wait_ge(z_ready, n0 + t + 1)
                    for a in range(2):
                        last = nc.tensor.transpose(zTP[a][:, t * P:t * P + P], zA[:, t, a * DH:a * DH + DH], identf[:])
                last.then_inc(zT_done, 1)
                if following:
                    convolve_tiles(*following, range(GRP - 1, GRP))
                cols = tiles * P
                pe.wait_ge(zT_copied, g * 2 + 4)
                for which in range(2):
                    pe.wait_ge(rest_ready, g * 2 + which + 1)
                    for a in range(2):
                        last = mm(qkP[which][:, 0:cols], wqkv[0:DH + a, a, which, :], zT[0:DH + a, a, 0:cols],
                                  start=a == 0, stop=a == 1)
                    last.then_inc(qk_done, 1)
                pe.wait_ge(v_copied, g + 1)
                for t in range(tiles):
                    for a in range(2):
                        last = mm(vP[:, t, :], zT[0:DH + a, a, t * P:t * P + P], wqkv[0:DH + a, a, 2, :],
                                  start=a == 0, stop=a == 1)
                last.then_inc(v_done, 1)

            def convolve_and_qkv(g, following):
                convolve_tiles(*following, range(GRP - 1))
                qkv_group(g, GRP, following)

            convolve_tiles(0, 0, 0, range(GRP))
            pe.wait_ge(const_step, CONSTANTS)
            pe.wait_ge(weights_step, FOLD_STEPS)
            with pe.Fori(0, B - 1) as b:
                for half in range(HALVES):
                    g = b * HALVES + half
                    convolve_and_qkv(g, (g + 1, 1 - half, b + half))
            convolve_and_qkv(NGRP - HALVES, (NGRP - 1, 1, B - 1))
            qkv_group(NGRP - 1, GRP)
            qkv_group(NGRP, TXT_TILES)
            pe.wait_ge(weights_step, SUM_STEPS)
            mm(wsumP[:, 0:1], ones[0:DH, :], wsum[0:DH, 0:1], start=True, stop=True)
            mm(wsumP[:, 1:2], ones[:], wsum[:, 1:2], start=True, stop=True).then_inc(wsum_done, 1)
            pe.wait_ge(weights_step, WEIGHT_STEPS)

            def row_scores(seq, par, u):
                i, k0, w = S1_USES[u]
                rows = P if i < NT else NTXT
                place = s1P[u % RING2]
                pe.wait_ge(s1_read, seq * NS1 + u + 1)
                if u < RING2:
                    pe.wait_ge(maxT_in, seq * 2 + u + 1)
                if rows < P:
                    own_wait(pe)
                diag = P * i - k0 if i < NT or k0 else None
                for c in range(0, w, 512):
                    cw = min(512, w - c)
                    last = mm(place[0:rows, c:c + cw], qs[0:MROW, par, P * i:P * i + rows],
                              ks[0:MROW, par, k0 + c:k0 + c + cw], start=True, stop=True, skip_group_check=True)
                    if diag is not None and c <= diag < c + cw:
                        last = mm(place[0:rows, diag:diag + rows], tri[0:rows, 0:rows], ident[0:rows, 0:rows],
                                  start=False, stop=True, skip_group_check=True)
                last.then_inc(s1_done, 1)

            def maxima_as_rows(seq):
                pe.wait_ge(parts_ready, seq + 1)
                for t in range(NT):
                    last = mm(s1P[0][MROW:MROW + 3, P * t:P * t + P], nmparts[:, t, :], ident[:], start=True, stop=True)
                last.then_inc(maxT_done, 1)
                mm(s1P[1][MROW:MROW + 3, 0:NTXT], nmparts[0:NTXT, NT, :], ident[0:NTXT, 0:NTXT], start=True, stop=True
                   ).then_inc(maxT_done, 1)

            def times_v(seq, k, j):
                d, p = low_counts(DONE_AT[j] - 1)
                pe.wait_ge(lo_by_dve, seq * len(DVE_CHUNKS) + d + RING5)
                pe.wait_ge(lo_by_pool, seq * len(POOL_CHUNKS) + p + RING5)
                keys = P if j < NT else NTXT
                if j == NT:
                    pe.wait_ge(av_read, seq + 1)
                    own_wait(pe)
                for r, (q0, w) in enumerate(RUNS):
                    lo = max(P * j, q0)
                    if lo >= q0 + w:
                        continue
                    cols = slice(POFF[j] + lo - P * j, POFF[j] + q0 + w - P * j)
                    opening = j == (q0 + w - 1) // P
                    for part in (whi, wlo):
                        last = mm(avP[32 * r:32 * r + VW * VP, lo - q0:w], vs[0:keys, k, j, :], part[0:keys, cols],
                                  start=opening and part is whi, stop=True, skip_group_check=True)
                return last

            def scores_and_products(seq, k, lap, first, last):
                nxt = (k + 1) % RING3
                pe.wait_ge(maxT_in, seq * 2 + 2 + 2)
                if not last:
                    pe.wait_ge(qkv_loaded[nxt], (lap + (k + 1) // RING3) * 64 + 64)
                for n, (j, a, w) in enumerate(CHUNKS):
                    keys = P if j < NT else NTXT
                    place = s2P[n % RING3]
                    pe.wait_ge(exp_done, seq * NS2 + n + 1)
                    if keys < P:
                        own_wait(pe)
                    done = mm(place[0:keys, 0:w], ks[0:KALL, k, P * j:P * j + keys],
                              qs[0:KALL, k, P * j + a:P * j + a + w], start=True, stop=True, skip_group_check=True)
                    if a == 0:
                        done = mm(place[0:keys, 0:keys], ident[0:keys, 0:keys], tri[0:keys, 0:keys],
                                  start=False, stop=True, skip_group_check=True)
                    done.then_inc(s2_done, 1)
                    if not last:
                        for u in S1_AFTER.get(n, ()):
                            row_scores(seq + 1, nxt, u)
                        if n == NS2 - 1:
                            maxima_as_rows(seq + 1)
                    if not first:
                        for jj in BEHIND_AFTER.get(n, ()):
                            times_v(seq - 1, (k - 1) % RING3, jj).then_inc(av_step, 1)
                    for jj in AV_AFTER.get(n, ()):
                        times_v(seq, k, jj).then_inc(av_step, 1)
                if last:
                    for jj in (1, 0):
                        times_v(seq, k, jj).then_inc(av_step, 1)

            pe.wait_ge(qkv_loaded[0], 64)
            for u in range(NS1):
                row_scores(0, 0, u)
            maxima_as_rows(0)
            stage_b(scores_and_products, pe)

            def project(b, k, lap):
                pe.wait_ge(batch_loaded[k], lap * 64 + 64)
                for c in range(3):
                    n = b * 3 + c
                    pe.wait_ge(cxn_ready, n + 1)
                    mm(spreadP[c], spread[:, k, :], rsums[:, c * (S // 3):(c + 1) * (S // 3)], start=True, stop=True
                       ).then_inc(spread_done, 1)
                pe.wait_ge(cxn_ready, b * 3 + 3 + 3)
                for t in range(NTT):
                    n = b * NTT + t
                    rows = P if t < NT else NTXT
                    pe.wait_ge(h2_ready, n + 1)
                    mm(projP[t % RING3][0:rows], cxn[:, P * t:P * t + rows], wout[:], start=True, stop=True
                       ).then_inc(proj_done, 1)

            pe.wait_ge(rsums_ready, 1)
            with pe.Fori(0, B // RING2) as i:
                for k in range(RING2):
                    project(i * RING2 + k, k, i)
            pe.wait_ge(h2_ready, B * NTT + RING3)

            def up_group(g):
                pe.wait_ge(x1T_copied, g + 1)
                for k in range(CGRP):
                    pe.wait_ge(ints1, g * CGRP + k + 1)
                    for a in range(2):
                        last = nc.tensor.transpose(x1TP[:, a, k * P:k * P + P], xqC[:, k, a * DH:a * DH + DH], ident[:])
                last.then_inc(x1T_done, 1)
                pe.wait_ge(x1T_copied, g + 2)
                for k in range(CGRP):
                    pe.wait_ge(gelu_done, g * CGRP + k + 1 - SINCE[k] + CGRP)
                    for half in range(2):
                        for a in range(2):
                            last = mm(upP[TWO_PLACES[k]][:, half, :], x1T[:, a, k * P:k * P + P],
                                      w1q[:, a, half * UPW:half * UPW + UPW], start=a == 0, stop=a == 1)
                    last.then_inc(up_done, 1)

            def down_tile(g, k):
                n = g * CGRP + k
                pe.wait_ge(x2T_copied, n + 1 + CGRP)
                if k == 0:
                    pe.wait_ge(out_done, g * CGRP + 2)
                if k == 2:
                    pe.wait_ge(out_done, g * CGRP + CGRP)
                    if left(g):
                        pe.wait_ge(gelu_done, (g + 2) * CGRP + CGRP)
                for f in range(FT):
                    last = mm(downP[k], x2T[:, k, f, :], w2q[:, f, :], start=f == 0, stop=f == FT - 1)
                last.then_inc(down_done, 1)

            def up_and_down(g, r, lap):
                if left(g):
                    up_group(g + 1)
                for k in range(CGRP):
                    n = g * CGRP + k
                    pe.wait_ge(ints2, n + 1 + RING3 * CGRP)
                    pe.wait_ge(x2T_copied, n + 1 - SINCE[k] + CGRP)
                    for f in range(FT):
                        last = nc.tensor.transpose(x2TP[TWO_PLACES[k]][:, f, :], xqF[:, k, f * P:f * P + P], ident[:])
                    last.then_inc(x2T_done, 1)
                    if k:
                        down_tile(g, k - 1)
                down_tile(g, CGRP - 1)

            up_group(0)
            stage_c(pe, up_and_down)


def kernel(**inputs):
    import concourse.bacc as bacc
    from concourse.bass_utils import run_bass_kernel_spmd

    a = {name: np.asarray(value) for name, value in inputs.items()}

    def tiles(x, rows):
        return np.ascontiguousarray(x.reshape(x.shape[0] // rows, rows, -1).transpose(1, 0, 2))

    side = SIDE * PATCH
    patches = a["x"][:, :, :side, :side].reshape(B, C_IN, SIDE, PATCH, SIDE, PATCH)
    patches = patches.transpose(1, 3, 5, 0, 2, 4).reshape(KT, P, NGRP, W)
    pos_ids = patch_positions()
    w_back = np.zeros((D, H, VW), np.float32)
    w_back[:, :, 0:HD] = a["L0_attn_W_back"].T.reshape(D, H, HD)
    spread_rows = np.zeros((B, H, B, H, VW), np.float32)
    for b in range(B):
        for h in range(H):
            spread_rows[b, h, b, h, :] = 1.0
    spread_rows = np.ascontiguousarray(spread_rows.reshape(HEADS, B, CR).transpose(1, 0, 2))
    arrays = {
        "xT": np.ascontiguousarray(patches.transpose(2, 1, 0, 3)),
        "idx": np.ascontiguousarray(a["x_txt"].reshape(TXT_TILES, P).T),
        "conv_w": tiles(a["L0_tok_conv_w"].reshape(D, KC).T, P),
        "conv_b": a["L0_tok_conv_b"],
        "pos": tiles(a["L0_tok_pos_table"][pos_ids], P),
        "emb": np.ascontiguousarray(a["L0_txt_weight"].T),
        "w_attn": tiles(np.concatenate([a["L0_attn_W_attn"].T, a["L0_attn_b_attn"][:, None]], axis=1), DH),
        "p_q": tiles(a["L0_attn_P_q"], DH),
        "p_k": tiles(a["L0_attn_P_k"], DH),
        "p_v": tiles(a["L0_attn_P_v"], DH),
        "w_back": tiles(w_back.reshape(D, CR), DH),
        "w_proj": tiles(a["L0_attn_W_proj"], DH),
        "b_proj": a["L0_attn_b_proj"].reshape(1, D),
        "spread_rows": spread_rows,
        "row_of_ones": np.ones((1, S), np.float32),
        "w1": tiles(a["L0_ffn_w1"].T, DH),
        "g1": a["L0_ffn_g1"],
        "w2": tiles(a["L0_ffn_w2"].T, P),
        "g2": a["L0_ffn_g2"],
    }
    nc = bacc.Bacc("TRN2", target_bir_lowering=False, num_devices=1)
    args = [nc.dram_tensor(f"in_{name}", x.shape, mybir.dt.from_np(x.dtype), kind="ExternalInput").ap()
            for name, x in arrays.items()]
    args.append(nc.dram_tensor("out_tokens", (TOK, D), F32, kind="ExternalOutput").ap())
    early_fusion_kernel(nc, *args)
    r = run_bass_kernel_spmd(nc, [{f"in_{name}": x for name, x in arrays.items()}], core_ids=[0])
    return r.results[0]["out_tokens"].reshape(B, S, D)


def patch_positions():
    boundaries = np.arange(1.0 / SIDE, 1.0, 1.0 / SIDE, dtype=np.float32)
    frac = np.arange(0.0, 1.0 - 1e-06, 1.0 / SIDE, dtype=np.float32)
    at = np.searchsorted(boundaries, frac, side="right")
    return (at[:, None] * SIDE + at).reshape(-1)
```
